# Optimizing a Trainium2 kernel written in Bass

```python
import numpy as np
import jax
import jax.numpy as jnp

def _softmax(x, axis=-1):
    return jax.nn.softmax(x, axis=axis)

def _gelu(x):
    return jax.nn.gelu(x, approximate=True)

def _silu(x):
    return jax.nn.silu(x)

def _sigmoid(x):
    return jax.nn.sigmoid(x)

def _layernorm(x, axis=-1, eps=1e-05):
    m = jnp.mean(x, axis=axis, keepdims=True)
    v = jnp.var(x, axis=axis, keepdims=True)
    return (x - m) / jnp.sqrt(v + eps)

def _scatter_add(tgt, idx, src, axis=0):
    return tgt.at[idx].add(src)

def _segment_sum(src, seg, n):
    return jax.ops.segment_sum(src, seg, n)
kernel_name = 'mk_lm_tower_d1_tok_ids1024_r4_716155'

def setup_inputs(seed: int=0):
    np.random.seed(seed)
    _w = jnp.asarray

    def _rec_inputs():
        import jax
        import jax.numpy as jnp
        _rk = jax.random.key(seed)
        x = jax.random.randint(jax.random.fold_in(_rk, 1), (16, 128), 0, 30521, jnp.int32)
        mask_BS_i1_0 = jnp.where(jnp.ones((16, 128), dtype=bool), 1, 0).astype(jnp.int32)
        return (x, mask_BS_i1_0)
    x, mask_BS_i1_0 = _rec_inputs()

    def _L0_tok_setup():
        import jax, jax.numpy as jnp
        import numpy as np
        LN_EPS = 1e-12
        key = jax.random.key(seed)
        k1, k2, k3, k4, k5 = jax.random.split(key, 5)
        B, S, H, V, P, T = (32, 128, 256, 30522, 128, 2)
        input_ids = jax.random.randint(k1, (B, S), 0, V, dtype=jnp.int64)
        token_type_ids = jax.random.randint(k2, (B, S), 0, T, dtype=jnp.int64)
        word_emb = jax.random.normal(k3, (V, H), dtype=jnp.float32) * 0.02
        pos_emb = jax.random.normal(k4, (P, H), dtype=jnp.float32) * 0.02
        type_emb = jax.random.normal(k5, (T, H), dtype=jnp.float32) * 0.02
        gamma = jnp.ones((H,), dtype=jnp.float32)
        beta = jnp.zeros((H,), dtype=jnp.float32)
        return {'input_ids': input_ids, 'token_type_ids': token_type_ids, 'word_emb': word_emb, 'pos_emb': pos_emb, 'type_emb': type_emb, 'gamma': gamma, 'beta': beta}
    _L0_tok_all = _L0_tok_setup()
    _L0_tok_in = {k: v for k, v in _L0_tok_all.items() if k in ('word_emb', 'pos_emb', 'type_emb', 'gamma', 'beta')}
    del _L0_tok_all

    def _L0_attn_setup():
        import jax, jax.numpy as jnp
        import numpy as np
        import math
        HEADS = 16
        LN_EPS = 1e-05

        def _layernorm(x, w, b):
            mu = jnp.mean(x, axis=-1, keepdims=True)
            var = jnp.mean((x - mu) ** 2, axis=-1, keepdims=True)
            return (x - mu) * jax.lax.rsqrt(var + LN_EPS) * w + b
        key = jax.random.key(seed)
        ks = jax.random.split(key, 8)
        b, t, e = (2, 512, 256)
        s = e // HEADS
        sc = 1.0 / math.sqrt(e)
        inp = {'x': jax.random.normal(ks[0], (b, t, e), dtype=jnp.float32), 'Wk': jax.random.normal(ks[1], (e, e), dtype=jnp.float32) * sc, 'Wq': jax.random.normal(ks[2], (e, e), dtype=jnp.float32) * sc, 'Wv': jax.random.normal(ks[3], (e, e), dtype=jnp.float32) * sc, 'Wo': jax.random.normal(ks[4], (e, e), dtype=jnp.float32) * sc, 'bo': jnp.zeros((e,), dtype=jnp.float32), 'kln_w': jnp.ones((s,), dtype=jnp.float32), 'kln_b': jnp.zeros((s,), dtype=jnp.float32), 'qln_w': jnp.ones((s,), dtype=jnp.float32), 'qln_b': jnp.zeros((s,), dtype=jnp.float32)}
        return inp
    _L0_attn_all = _L0_attn_setup()
    _L0_attn_in = {k: v for k, v in _L0_attn_all.items() if k in ('Wk', 'Wq', 'Wv', 'Wo', 'bo', 'kln_w', 'kln_b', 'qln_w', 'qln_b')}
    del _L0_attn_all

    def _L0_ffn_setup():
        import jax, jax.numpy as jnp
        import numpy as np
        TOP_K = 2
        NUM_EXPERTS = 8
        DIM = 256
        HIDDEN = 704
        BS, SLEN = (2, 256)

        def _grouped_ffn(x, w1, w2, w3, counts):
            num_experts = w1.shape[0]
            ends = jnp.cumsum(counts)
            starts = ends - counts
            t = jnp.arange(x.shape[0])
            out = jnp.zeros((x.shape[0], w2.shape[-1]), x.dtype)
            for e in range(num_experts):
                m = ((t >= starts[e]) & (t < ends[e])).astype(x.dtype)[:, None]
                xe = x * m
                h = jax.nn.silu(xe @ w1[e]) * (xe @ w3[e])
                out = out + h @ w2[e] * m
            return out
        key = jax.random.key(seed)
        k = jax.random.split(key, 5)
        std = 0.02
        return {'x': jax.random.normal(k[0], (BS, SLEN, DIM), jnp.float32), 'gate_w': jax.random.normal(k[1], (NUM_EXPERTS, DIM), jnp.float32) * std, 'expert_bias': jnp.zeros((NUM_EXPERTS,), jnp.float32), 'w1': jax.random.normal(k[2], (NUM_EXPERTS, DIM, HIDDEN), jnp.float32) * std, 'w2': jax.random.normal(k[3], (NUM_EXPERTS, HIDDEN, DIM), jnp.float32) * std, 'w3': jax.random.normal(k[4], (NUM_EXPERTS, DIM, HIDDEN), jnp.float32) * std}
    _L0_ffn_all = _L0_ffn_setup()
    _L0_ffn_in = {k: v for k, v in _L0_ffn_all.items() if k in ('gate_w', 'expert_bias', 'w1', 'w2', 'w3')}
    del _L0_ffn_all
    return {'x': x, 'mask_BS_i1_0': mask_BS_i1_0, 'L0_tok_word_emb': _L0_tok_in['word_emb'], 'L0_tok_pos_emb': _L0_tok_in['pos_emb'], 'L0_tok_type_emb': _L0_tok_in['type_emb'], 'L0_tok_gamma': _L0_tok_in['gamma'], 'L0_tok_beta': _L0_tok_in['beta'], 'L0_attn_Wk': _L0_attn_in['Wk'], 'L0_attn_Wq': _L0_attn_in['Wq'], 'L0_attn_Wv': _L0_attn_in['Wv'], 'L0_attn_Wo': _L0_attn_in['Wo'], 'L0_attn_bo': _L0_attn_in['bo'], 'L0_attn_kln_w': _L0_attn_in['kln_w'], 'L0_attn_kln_b': _L0_attn_in['kln_b'], 'L0_attn_qln_w': _L0_attn_in['qln_w'], 'L0_attn_qln_b': _L0_attn_in['qln_b'], 'L0_ffn_gate_w': _L0_ffn_in['gate_w'], 'L0_ffn_expert_bias': _L0_ffn_in['expert_bias'], 'L0_ffn_w1': _L0_ffn_in['w1'], 'L0_ffn_w2': _L0_ffn_in['w2'], 'L0_ffn_w3': _L0_ffn_in['w3']}

def reference(x, mask_BS_i1_0, L0_tok_word_emb, L0_tok_pos_emb, L0_tok_type_emb, L0_tok_gamma, L0_tok_beta, L0_attn_Wk, L0_attn_Wq, L0_attn_Wv, L0_attn_Wo, L0_attn_bo, L0_attn_kln_w, L0_attn_kln_b, L0_attn_qln_w, L0_attn_qln_b, L0_ffn_gate_w, L0_ffn_expert_bias, L0_ffn_w1, L0_ffn_w2, L0_ffn_w3):
    import jax
    import jax.numpy as jnp

    def _L0_tok_ref(input_ids, token_type_ids, word_emb, pos_emb, type_emb, gamma, beta):
        import jax, jax.numpy as jnp
        import numpy as np
        LN_EPS = 1e-12
        S = input_ids.shape[1]
        x = word_emb[input_ids] + pos_emb[jnp.arange(S)][None] + type_emb[token_type_ids]
        mu = jnp.mean(x, axis=-1, keepdims=True)
        var = jnp.mean(jnp.square(x - mu), axis=-1, keepdims=True)
        x = (x - mu) / jnp.sqrt(var + LN_EPS)
        return gamma * x + beta

    def _L0_attn_ref(x, Wk, Wq, Wv, Wo, bo, kln_w, kln_b, qln_w, qln_b):
        import jax, jax.numpy as jnp
        import numpy as np
        import math
        HEADS = 16
        LN_EPS = 1e-05

        def _layernorm(x, w, b):
            mu = jnp.mean(x, axis=-1, keepdims=True)
            var = jnp.mean((x - mu) ** 2, axis=-1, keepdims=True)
            return (x - mu) * jax.lax.rsqrt(var + LN_EPS) * w + b
        b, t, e = x.shape
        h = HEADS
        s = e // h
        scale = 1.0 / math.sqrt(s)
        k = (x @ Wk).reshape(b, t, h, s)
        q = (x @ Wq).reshape(b, t, h, s)
        v = (x @ Wv).reshape(b, t, h, s)
        k = _layernorm(k, kln_w, kln_b)
        q = _layernorm(q, qln_w, qln_b)
        dot = jnp.einsum('bqhs,bkhs->bhqk', q, k) * scale
        causal = jnp.tril(jnp.ones((t, t), dtype=bool))
        dot = jnp.where(causal, dot, -jnp.inf)
        attn = jax.nn.softmax(dot, axis=-1)
        out = jnp.einsum('bhqk,bkhs->bqhs', attn, v).reshape(b, t, e)
        return out @ Wo + bo

    def _L0_ffn_ref(x, gate_w, expert_bias, w1, w2, w3):
        import jax, jax.numpy as jnp
        import numpy as np
        TOP_K = 2
        NUM_EXPERTS = 8
        DIM = 256
        HIDDEN = 704
        BS, SLEN = (2, 256)

        def _grouped_ffn(x, w1, w2, w3, counts):
            num_experts = w1.shape[0]
            ends = jnp.cumsum(counts)
            starts = ends - counts
            t = jnp.arange(x.shape[0])
            out = jnp.zeros((x.shape[0], w2.shape[-1]), x.dtype)
            for e in range(num_experts):
                m = ((t >= starts[e]) & (t < ends[e])).astype(x.dtype)[:, None]
                xe = x * m
                h = jax.nn.silu(xe @ w1[e]) * (xe @ w3[e])
                out = out + h @ w2[e] * m
            return out
        bs, slen, dim = x.shape
        num_experts = gate_w.shape[0]
        xf = x.reshape(bs * slen, dim)
        scores = jax.nn.softmax((xf @ gate_w.T).astype(jnp.float32), axis=-1)
        _, sel = jax.lax.top_k(scores + expert_bias, TOP_K)
        top_scores = jnp.take_along_axis(scores, sel, axis=1).reshape(-1)
        sel_flat = sel.reshape(-1)
        counts = jnp.zeros((num_experts,), jnp.int32).at[sel_flat].add(1)
        order = jnp.argsort(sel_flat, stable=True)
        top_scores_sorted = top_scores[order]
        token_idx = order // TOP_K
        routed = xf[token_idx] * top_scores_sorted[:, None].astype(xf.dtype)
        routed_out = _grouped_ffn(routed, w1, w2, w3, counts)
        out = jnp.zeros_like(xf).at[token_idx].add(routed_out)
        return out.reshape(bs, slen, dim)
    h = _L0_tok_ref(x, mask_BS_i1_0, L0_tok_word_emb, L0_tok_pos_emb, L0_tok_type_emb, L0_tok_gamma, L0_tok_beta)
    h = h + _L0_attn_ref(_layernorm(h, axis=-1), L0_attn_Wk, L0_attn_Wq, L0_attn_Wv, L0_attn_Wo, L0_attn_bo, L0_attn_kln_w, L0_attn_kln_b, L0_attn_qln_w, L0_attn_qln_b)
    h = h + _L0_ffn_ref(_layernorm(h, axis=-1), L0_ffn_gate_w, L0_ffn_expert_bias, L0_ffn_w1, L0_ffn_w2, L0_ffn_w3)
    return h

_drawn_inputs = setup_inputs


def setup_inputs(seed=0):
    import zlib

    import numpy as np

    out = dict(_drawn_inputs(seed))
    spreads = {'L0_tok_gamma': (1.0, 0.2),
     'L0_tok_beta': (0.0, 0.1),
     'L0_attn_bo': (0.0, 0.1),
     'L0_attn_kln_w': (1.0, 0.2),
     'L0_attn_kln_b': (0.0, 0.8),
     'L0_attn_qln_w': (1.0, 0.6),
     'L0_attn_qln_b': (0.0, 0.8),
     'L0_ffn_expert_bias': (0.0, 0.8)}
    factors = {'L0_ffn_gate_w': 8.0, 'L0_ffn_w1': 8.0, 'L0_ffn_w2': 8.0, 'L0_ffn_w3': 8.0}
    for name, (base, spread) in spreads.items():
        noise = np.random.default_rng([zlib.crc32(name.encode()), seed]).standard_normal(out[name].shape)
        drawn = base * np.exp(spread * noise) if base else spread * noise
        out[name] = jnp.asarray(drawn.astype(out[name].dtype))
    for name, factor in factors.items():
        out[name] = (out[name] * factor).astype(out[name].dtype)
    return out
```

```python
from contextlib import ExitStack

import concourse.bass as bass
import concourse.mybir as mybir

P = 128
B = 16
D = 256
DK = D // P
H = 16
HD = D // H
HP = 32
GROUPS = H * HP // P
RG = P // HP
E = 8
F = 704
FH = F // 2
FK = -(-F // P)
FT = F - (FK - 1) * P
TOK = B * P
TOPK = 2
NT = (TOK * TOPK + E * (P - 1)) // P
NTP = NT + 1
RB = TOK // P
TROWS = E * RB + NTP - TOK * TOPK // P
VW = HD + 1
NEG = -1.0e30
QK_BANK, VY_BANK, T_BANK, O_BANK = 4, 5, 6, 7
MT_AT, GATE_AT, RANK_AT = 288, 360, 368


def spread(ap, axis, count):
    ap = ap.unsqueeze(axis)
    shape = list(ap.shape)
    shape[axis] = count
    return ap.broadcast_to(shape)


def build_tower(nc, ids, types, word, rows, w_qkv, w_o, head_cols, gate_t, w1, w3, w2, out):
    f32, bf16, i32, u32 = mybir.dt.float32, mybir.dt.bfloat16, mybir.dt.int32, mybir.dt.uint32
    ALU, ACT, AX = mybir.AluOpType, mybir.ActivationFunctionType, mybir.AxisListType

    x2_dram = nc.dram_tensor("x2_rows", (TOK, D), f32).ap()
    table = nc.dram_tensor("slot_table", (TROWS * P, 2), f32).ap()
    y_dram = nc.dram_tensor("expert_rows", (TOPK * TOK + P, D), f32).ap()

    ctx = ExitStack()
    with ctx:
        def sb(name, shape, dt=f32):
            return ctx.enter_context(nc.sbuf_tensor(name, shape, dt))

        def sem(name):
            return ctx.enter_context(nc.semaphore(name))

        w13_sb = sb("w13_sb", [P, E, DK, 2 * F])
        w2_sb = sb("w2_sb", [P, E, FK, D])
        h_all = sb("h_all", [P, B, D])
        wo_sb = sb("wo_sb", [P, DK, D])
        rows_sb = sb("rows_sb", [P, 7, D])
        gate_sb = sb("gate_sb", [P, DK, E])
        cols_sb = sb("cols_sb", [P, 4])
        ids_sb = sb("ids_sb", [P, B], i32)
        types_sb = sb("types_sb", [P, B], i32)
        typesf = sb("typesf", [P, B])
        ident = sb("ident", [P, P])
        identb = sb("identb", [P, P], bf16)
        upper = sb("upper", [P, P], bf16)
        onesb = sb("onesb", [P, P], bf16)
        mask_qk = sb("mask_qk", [P, P], bf16)
        mask_kq = sb("mask_kq", [P, P], bf16)
        sel = sb("sel", [3 * H, H, P], bf16)
        neghalf = sb("neghalf", [P, 2 * H])
        iota_e = sb("iota_e", [P, E])
        slot_base = sb("slot_base", [P, E])
        dest_all = sb("dest_all", [P, B, TOPK])
        prep = sb("prep", [P, 2 * DK * H])
        idx = [sb(f"idx{p}", [P, 1], i32) for p in range(2)]
        tcol = sb("tcol", [P, 1])
        zeros = sb("zeros", [P, TOPK])
        x_in = [sb(f"x_in{p}", [P, D]) for p in range(2)]
        x_base = sb("x_base", [P, D])
        tmp = sb("tmp", [P, D])
        st6 = sb("st6", [P, 3, 6])
        mv = sb("mv", [P, 3, 2])
        veps = sb("veps", [P, 3])
        rstd = sb("rstd", [P, 3])
        a_n = [sb(f"a_n{p}", [P, D]) for p in range(2)]
        aT = sb("aT", [P, DK, P])
        v_aug = [sb(f"v_aug{p}", [P, H, VW]) for p in range(2)]
        ss = sb("ss", [P, 2 * H])
        sse = sb("sse", [P, 2 * H])
        rqk = sb("rqk", [P, 2 * H])
        qkn = sb("qkn", [P, 2 * H, HP])
        nmax = sb("nmax", [P, H])
        nres = sb("nres", [P, H])
        m3 = sb("m3", [P, P // H, H], bf16)
        mT = sb("mT", [3 * H, P], bf16)
        work = [sb(f"work{p}", [P, 4 * 512]) for p in range(2)]
        rden = sb("rden", [P, H])
        oT = sb("oT", [P, DK, P])
        x2 = [sb(f"x2_{p}", [P, D]) for p in range(2)]
        x2T = sb("x2T", [P, DK, P])
        gneg = sb("gneg", [P, 1])
        gexp = sb("gexp", [P, E])
        gsum = sb("gsum", [P, 1])
        grs = sb("grs", [P, 1])
        score = sb("score", [P, E])
        biased = sb("biased", [P, E])
        top8 = sb("top8", [P, 8])
        topi = sb("topi", [P, 8], u32)
        topf = sb("topf", [P, TOPK])
        oh0 = sb("oh0", [P, E])
        junk = sb("junk", [P, 2, E])
        chosen = [sb(f"chosen{p}", [P, E], bf16) for p in range(2)]
        chosen_sum = [sb(f"chosen_sum{p}", [P, E], bf16) for p in range(2)]
        ranked = sb("ranked", [P, E])
        slotf = [sb(f"slotf{p}", [P, TOPK]) for p in range(2)]
        sloti = [sb(f"sloti{p}", [P, TOPK], i32) for p in range(2)]
        entry = [sb(f"entry{p}", [P, TOPK, 2]) for p in range(2)]
        steps16 = sb("steps16", [P, RB])
        ntile = sb("ntile", [P, 4, E])
        tile_no = sb("tile_no", [P, 1])
        tile_row = sb("tile_row", [1, NTP])
        ended = sb("ended", [P, 2, E])
        erow = sb("erow", [P, 4])
        rowi = sb("rowi", [P, 1], i32)
        er = sb("er", [1, 2, NTP])
        er_i = sb("er_i", [1, NTP], i32)
        dest = sb("dest", [P, 3, NTP])
        dest_i = sb("dest_i", [P, NTP], i32)
        src_i = sb("src_i", [P, NTP], i32)
        slot_score = sb("slot_score", [P, NTP])
        src_c = [sb(f"src_c{p}", [P, 1], i32) for p in range(2)]
        dst_c = [sb(f"dst_c{p}", [P, 1], i32) for p in range(2)]
        PS = ctx.enter_context(nc.psum_tensor("PS", [P, 8, 512], f32))

        wqkv_sb = w2_sb[:, E - 1, :, :].rearrange("p k d -> p (k d)").rearrange("p (k n) -> p k n", k=DK)
        late = w13_sb[:, E - 1, :, :].rearrange("p k n -> p (k n)")
        qT, kT = ([late[:, (2 * i + p) * 512:(2 * i + p + 1) * 512].rearrange("p (g s) -> p g s", s=P)
                   for p in range(2)] for i in range(2))
        sq, o_n = late[:, 2048:2560], late[:, 2560:2816]
        over = work[1][:, 0:E * RB].rearrange("p (e j) -> p e j", e=E)
        le8 = work[1][0:1, 128:128 + NTP * E].rearrange("p (t e) -> p t e", e=E)
        trow = work[1][0:NTP, 512:512 + 2 * P].rearrange("p (s c) -> p s c", c=2)

        pos_t0, type_diff = rows_sb[:, 0, :], rows_sb[:, 2, :]
        gamma, beta, bo = rows_sb[:, 3, :], rows_sb[:, 4, :], rows_sb[:, 5, :]
        ebias = rows_sb[:, 6, 0:E]
        mT_ps = PS[:, O_BANK, MT_AT:MT_AT + P // 2].bitcast(bf16)
        init_rows = work[0][:, 0:2 * P].rearrange("p (s c) -> p s c", c=2)

        def part(p, at, n):
            return work[p][:, at:at + n]
        XG, XT, HH, HT = 0, 256, 512, 512 + F
        hT_sb = [part(p, HT, FK * P).rearrange("p (k s) -> p k s", k=FK) for p in range(2)]
        h_sb = [part(p, HH, F) for p in range(2)]
        xg_sb = [part(p, XG, D) for p in range(2)]
        xT_sb = [part(p, XT, D).rearrange("p (k s) -> p k s", k=DK) for p in range(2)]
        y_sb = x_in
        CH = 4
        y_back = [w13_sb[:, c, :, 0:1024].rearrange("p k (t d) -> p k t d", d=D) for c in range(B // CH)]

        ld_small, ld_qkv, ld_ffn = sem("ld_small"), sem("ld_qkv"), sem("ld_ffn")
        pool_const, pool_step = sem("pool_const"), sem("pool_step")
        prep_done, prep_step = sem("prep_done"), sem("prep_step")
        table_init = sem("table_init")
        gathered = [sem(f"gathered{p}") for p in range(2)]
        pool_chain, dve_chain = sem("pool_chain"), sem("dve_chain")
        x_base_ready, x_summed, pool_bo = sem("x_base_ready"), sem("x_summed"), sem("pool_bo")
        var_e, var_a, var_f, var_qk = sem("var_e"), sem("var_a"), sem("var_f"), sem("var_qk")
        rstd_e, rstd_a, rstd_f, rstd_qk = sem("rstd_e"), sem("rstd_a"), sem("rstd_f"), sem("rstd_qk")
        x_used, a_ready = sem("x_used"), sem("a_ready")
        m3_ready, chosen_ready, slot_ready = sem("m3_ready"), sem("chosen_ready"), sem("slot_ready")
        aT_ps, aT_ready, qkv_done, v_ready, sq_ready = (
            sem("aT_ps"), sem("aT_ready"), sem("qkv_done"), sem("v_ready"), sem("sq_ready"))
        qkn_ready, q_ps, k_ps, q_ready, k_ready = (
            sem("qkn_ready"), sem("q_ps"), sem("k_ps"), sem("q_ready"), sem("k_ready"))
        s_done, max_done, mT_tr, mT_ready = (
            sem("s_done"), sem("max_done"), sem("mT_tr"), sem("mT_ready"))
        st_done, exp_done, pv_done, o_ready = sem("st_done"), sem("exp_done"), sem("pv_done"), sem("o_ready")
        oT_ps, oT_ready, wo_done = sem("oT_ps"), sem("oT_ready"), sem("wo_done")
        x2_ready, x2T_ps, x2T_ready = sem("x2_ready"), sem("x2T_ps"), sem("x2T_ready")
        x2_stored = [sem(f"x2_stored{p}") for p in range(2)]
        gate_done, gneg_ready, gexp_ready = sem("gate_done"), sem("gneg_ready"), sem("gexp_ready")
        rank_done, sum_ready = sem("rank_done"), sem("sum_ready")
        scattered = [sem(f"scattered{p}") for p in range(2)]
        counts_done, rowi_ready, route_step, er_ready = (
            sem("counts_done"), sem("rowi_ready"), sem("route_step"), sem("er_ready"))
        trow_loaded, tab_tr, slots_ready = sem("trow_loaded"), sem("tab_tr"), sem("slots_ready")
        xg_loaded = [sem(f"xg_loaded{p}") for p in range(2)]
        xs_ready, xT_tr, xT_ready = sem("xs_ready"), sem("xT_tr"), sem("xT_ready")
        w13_done, silu_ready, hh_ready = sem("w13_done"), sem("silu_ready"), sem("hh_ready")
        hT_tr, hT_a_ready, hT_v_ready = sem("hT_tr"), sem("hT_a_ready"), sem("hT_v_ready")
        w2_done, y_ready = sem("w2_done"), sem("y_ready")
        y_stored = [sem(f"y_stored{p}") for p in range(2)]
        y_loaded = [sem(f"y_loaded{c}") for c in range(B // CH)]
        sum_step, out_ready, out_stored = sem("sum_step"), sem("out_ready"), sem("out_stored")

        block = ctx.enter_context(nc.Block())

        def wait(eng, s, n):
            if isinstance(n, int):
                n = min(n, B)
                if n <= 0:
                    return
            eng.wait_ge(s, n)

        def chain(eng, s):
            k = [0]

            def link(ins):
                k[0] += 1
                ins.then_inc(s, 1)
                eng.wait_ge(s, k[0])

            def clear():
                eng.sem_clear(s)
            return link, clear

        AHEAD, BEHIND = 4, 2
        LOOP = 4

        def valid(t):
            return not isinstance(t, int) or 0 <= t < B

        def half(j, p, ahead):
            return j + (p + ahead) // 2

        def attention(eng, step):
            for t in range(-AHEAD, LOOP):
                step(t, t % 2, t // 2)
            with eng.Fori(LOOP // 2, (B - AHEAD) // 2) as j:
                for p in range(2):
                    step(2 * j + p, p, j)
            for t in range(B - AHEAD, B + BEHIND):
                step(t, t % 2, t // 2)

        def experts(eng, first, loop_first, step):
            for t in range(first, loop_first):
                step(t, t % 2, (t - 1) // 2)
            with eng.Fori((loop_first - 1) // 2, (NT - 1) // 2) as j:
                for i in range(2):
                    step(2 * j + 1 + i, 1 - i, j)

        @block.sync
        def _(sp):
            sp.dma_start(ids_sb[:, :], ids).then_inc(ld_small, 16)
            sp.dma_start(types_sb[:, :], types).then_inc(ld_small, 16)
            sp.dma_start(rows_sb[:, 0, :], rows[0:P, :]).then_inc(ld_small, 16)
            sp.dma_start(rows_sb[:, 1:7, :],
                         spread(rows[P:P + 6, :], 0, P)).then_inc(ld_small, 16)
            sp.dma_start(cols_sb[:, :], head_cols).then_inc(ld_small, 16)
            sp.dma_start(wqkv_sb[:, :, :], w_qkv.rearrange("(k p) n -> p k n", p=P)).then_inc(ld_qkv, 16)
            sp.dma_start(wo_sb[:, :, :], w_o.rearrange("(k p) n -> p k n", p=P)).then_inc(ld_qkv, 16)
            sp.dma_start(gate_sb[:, :, :], gate_t.rearrange("(k p) n -> p k n", p=P)).then_inc(ld_qkv, 16)
            sp.wait_ge(pool_const, 1)
            sp.dma_start(table[0:P * P, :].rearrange("(r s) c -> r (s c)", s=P),
                         init_rows.rearrange("p s c -> p (s c)")).then_inc(table_init, 16)
            sp.dma_start(table[P * P:TROWS * P, :].rearrange("(r s) c -> r (s c)", s=P),
                         init_rows[0:TROWS - P].rearrange("p s c -> p (s c)")).then_inc(table_init, 16)
            def load_expert(e):
                sp.dma_start(w13_sb[:, e, :, 0:F], w1[e].rearrange("(k p) n -> p k n", p=P)).then_inc(ld_ffn, 16)
                sp.dma_start(w13_sb[:, e, :, F:2 * F], w3[e].rearrange("(k p) n -> p k n", p=P)).then_inc(ld_ffn, 16)
                sp.dma_start(w2_sb[:, e, 0:FK - 1, :],
                             w2[e, 0:F - FT].rearrange("(k p) n -> p k n", p=P)).then_inc(ld_ffn, 16)
                sp.dma_start(w2_sb[0:FT, e, FK - 1, :], w2[e, F - FT:F]).then_inc(ld_ffn, 16)

            for e in range(E - 1):
                load_expert(e)

            def store(t, p, j):
                u = t - 1
                if valid(u):
                    sp.wait_ge(x2_ready, u + 1)
                    sp.dma_start(x2_dram[bass.ds(u * P, P), :], x2[1 - p][:, :]).then_inc(x2_stored[1 - p], 16)
            attention(sp, store)

            sp.wait_ge(qkv_done, B)
            sp.wait_ge(var_qk, B)
            sp.wait_ge(st_done, RG * B)
            sp.wait_ge(oT_ps, B)
            load_expert(E - 1)

            sp.wait_ge(y_stored[0], 16 * (NT - NT // 2))
            sp.wait_ge(y_stored[1], 16 * (NT // 2))
            sp.wait_ge(w13_done, NT)
            for c in range(B // CH):
                for k in range(TOPK):
                    r0 = k * TOK + c * CH * P
                    sp.dma_start(y_back[c][:, k, :, :],
                                 y_dram[r0:r0 + CH * P, :].rearrange("(t p) d -> p t d", p=P)).then_inc(y_loaded[c], 16)
            for c in range(B // CH):
                sp.wait_ge(out_ready, c + 1)
                sp.dma_start(out[c * CH:(c + 1) * CH].rearrange("t p d -> p t d"),
                             h_all[:, c * CH:(c + 1) * CH, :]).then_inc(out_stored, 16)
            sp.wait_ge(out_stored, 16 * (B // CH))

        @block.gpsimd
        def _(pool):
            g = nc.gpsimd
            k = [0]

            def link(ins):
                k[0] += 1
                ins.then_inc(pool_step, 1)
                pool.wait_ge(pool_step, k[0])
            link(g.memset(init_rows, 0.0))
            g.iota(init_rows[:, :, 0], pattern=[[1, P]], base=TOPK * TOK, channel_multiplier=0,
                   allow_small_or_imprecise_dtypes=True).then_inc(pool_const, 1)
            g.memset(neghalf[:, :], -0.5)
            link(g.memset(ident[:, :], 0.0))
            link(g.affine_select(out=ident[:, :], in_=ident[:, :], compare_op=ALU.not_equal, fill=1.0,
                                 base=0, pattern=[[-1, P]], channel_multiplier=1))
            g.tensor_copy(identb[:, :], ident[:, :])
            g.memset(mask_qk[:, :], 0.0)
            g.memset(mask_kq[:, :], 0.0)
            link(g.memset(onesb[:, :], 1.0))
            g.affine_select(out=mask_qk[:, :], in_=mask_qk[:, :], compare_op=ALU.is_ge, fill=NEG,
                            base=0, pattern=[[-1, P]], channel_multiplier=1)
            g.affine_select(out=mask_kq[:, :], in_=mask_kq[:, :], compare_op=ALU.is_ge, fill=NEG,
                            base=0, pattern=[[1, P]], channel_multiplier=-1)
            g.affine_select(out=upper[:, :], in_=onesb[:, :], compare_op=ALU.is_gt, fill=0.0,
                            base=0, pattern=[[1, P]], channel_multiplier=-1)
            link(g.memset(sel[:, :, :], 0.0))
            for i in range(3):
                link(g.affine_select(out=sel[:, :, :], in_=sel[:, :, :], compare_op=ALU.not_equal, fill=1.0,
                                     base=-i * H, pattern=[[-1, H], [0, P]], channel_multiplier=1))
            exact = dict(allow_small_or_imprecise_dtypes=True)
            g.iota(iota_e[:, :], pattern=[[1, E]], base=0, channel_multiplier=0, **exact)
            g.iota(slot_base[:, :], pattern=[[TOK, E]], base=0, channel_multiplier=0, **exact)
            g.iota(dest_all[:, :, :], pattern=[[P, B], [TOK, TOPK]], base=0, channel_multiplier=1, **exact)
            g.iota(steps16[:, :], pattern=[[P, RB]], base=0, channel_multiplier=0, **exact)
            g.iota(tile_no[:, :], pattern=[[0, 1]], base=0, channel_multiplier=1, **exact)
            g.iota(tile_row[:, :], pattern=[[1, NTP]], base=0, channel_multiplier=0, **exact)
            for p in range(2):
                g.memset(v_aug[p][:, :, HD:VW], 1.0)
            g.memset(chosen_sum[0][:, :], 0.0)
            g.memset(zeros[:, :], 0.0)
            g.memset(m3[:, :, :], 0.0)
            g.memset(qkn[:, :, :], 0.0).then_inc(pool_const, 1)
            pool.wait_ge(prep_done, 1)

            def step(t, p, j):
                link, clear = chain(pool, pool_chain)
                u = t + 3
                if valid(u):
                    q = 1 - p
                    wait(pool, x_summed, u)
                    link(g.tensor_copy(tcol[:, :], typesf[:, bass.ds(u, 1)]))
                    link(g.tensor_scalar(x_base[:, :], type_diff, tcol[:, :], None, ALU.mult))
                    g.tensor_tensor(x_base[:, :], x_base[:, :], pos_t0, ALU.add).then_inc(x_base_ready, 1)
                u = t + 1
                if valid(u):
                    pool.wait_ge(var_qk, u + 1)
                    g.tensor_tensor(rqk[:, :], sse[:, :], neghalf[:, :], ALU.pow).then_inc(rstd_qk, 1)
                u = t + 3
                if valid(u):
                    for var, rs, c in ((var_e, rstd_e, 0), (var_a, rstd_a, 1)):
                        pool.wait_ge(var, u + 1)
                        g.tensor_tensor(rstd[:, c:c + 1], veps[:, c:c + 1], neghalf[:, 0:1], ALU.pow).then_inc(rs, 1)
                    pool.wait_ge(a_ready, u + 1)
                    hu = h_all[:, bass.ds(u, 1), :].rearrange("p o d -> p (o d)")
                    g.tensor_tensor(hu, hu, bo, ALU.add).then_inc(pool_bo, 1)
                u = t - 1
                if valid(u):
                    pool.wait_ge(var_f, u + 1)
                    g.tensor_tensor(rstd[:, 2:3], veps[:, 2:3], neghalf[:, 0:1], ALU.pow).then_inc(rstd_f, 1)
                u = t + 4
                if valid(u):
                    wait(pool, x_used, u - 1)
                    link(g.tensor_copy(idx[p][:, :], ids_sb[:, bass.ds(u, 1)]))
                    g.indirect_dma_start(x_in[p][:, :], None, word,
                                         bass.IndirectOffsetOnAxis(idx[p][:, :], 0)).then_inc(gathered[p], 16)
                u = t - 2
                if valid(u):
                    if isinstance(u, int) and u == 0:
                        pool.wait_ge(table_init, 32)
                    pool.wait_ge(slot_ready, u + 1)
                    link(g.tensor_tensor(slotf[p][:, :], slotf[p][:, :], zeros[:, :], ALU.add))
                    link(g.tensor_copy(sloti[p][:, :], slotf[p][:, :]))
                    for c in range(TOPK):
                        g.indirect_dma_start(table, bass.IndirectOffsetOnAxis(sloti[p][:, c:c + 1], 0),
                                             entry[p][:, c, :], None).then_inc(scattered[p], 16)
                clear()

            attention(pool, step)

            for p in range(2):
                pool.wait_ge(scattered[p], 16 * TOPK * B // 2)
            pool.wait_ge(rowi_ready, 1)
            g.indirect_dma_start(trow[:, :, :].rearrange("t s c -> t (s c)"), None,
                                 table.rearrange("(r s) c -> r (s c)", s=P),
                                 bass.IndirectOffsetOnAxis(rowi[0:NTP, :], 0)).then_inc(trow_loaded, 16)
            pool.wait_ge(slots_ready, 1)
            for p in range(2):
                pool.wait_ge(x2_stored[p], 16 * B // 2)

            def gather(t, p, link):
                link(g.tensor_copy(src_c[p][:, :], src_i[:, bass.ds(t, 1)]))
                g.indirect_dma_start(xg_sb[p], None, x2_dram,
                                     bass.IndirectOffsetOnAxis(src_c[p][:, :], 0)).then_inc(xg_loaded[p], 16)

            def scatter(t, p, link):
                pool.wait_ge(y_ready, t + 1)
                link(g.tensor_copy(dst_c[p][:, :], dest_i[:, bass.ds(t, 1)]))
                g.indirect_dma_start(y_dram, bass.IndirectOffsetOnAxis(dst_c[p][:, :], 0), y_sb[p][:, :],
                                     None).then_inc(y_stored[p], 16)

            def step(t, p, j):
                link, clear = chain(pool, pool_chain)
                pool.wait_ge(xT_tr, t)
                pool.wait_ge(xg_loaded[1 - p], 16 * j + 16)
                gather(t + 1, 1 - p, link)
                if not isinstance(t, int) or t > 2:
                    pool.wait_ge(y_stored[1 - p], 16 * j)
                if not isinstance(t, int) or t > 1:
                    pool.wait_ge(y_stored[p], 16 * (j + 1 - p))
                scatter(t - 1, 1 - p, link)
                clear()
            link, clear = chain(pool, pool_chain)
            gather(0, 0, link)
            gather(1, 1, link)
            clear()
            experts(pool, 1, 3, step)
            for p in range(2):
                pool.wait_ge(y_stored[p], 16 * (NT // 2))
            scatter(NT - 1, 0, chain(pool, pool_chain)[0])

        @block.scalar
        def _(act):
            a = nc.scalar

            def step(t, p, j):
                u = t + 1
                if valid(u):
                    act.wait_ge(qkv_done, u + 1)
                    wait(act, var_qk, u)
                    a.activation(sq[:, :], PS[:, QK_BANK, :], ACT.Square).then_inc(sq_ready, 1)
                    wait(act, pv_done, u - 1)
                    a.activation(v_aug[1 - p][:, :, 0:HD], PS[:, VY_BANK, 0:D].rearrange("p (h s) -> p h s", s=HD),
                                 ACT.Copy).then_inc(v_ready, 1)
                u = t - 2
                if valid(u):
                    act.wait_ge(x2T_ps, u + 1)
                    wait(act, gate_done, u)
                    a.activation(x2T[:, :, :].rearrange("p k s -> p (k s)"), PS[:, T_BANK, 0:D],
                                 ACT.Copy).then_inc(x2T_ready, 1)
                if valid(t):
                    wait(act, pv_done, t - 1)
                    for r in range(RG):
                        act.wait_ge(st_done, RG * t + r + 1)
                        a.activation(work[p][:, r * 512:(r + 1) * 512], PS[:, r, :], ACT.Exp,
                                     scale=HD ** -0.5).then_inc(exp_done, 1)
                u = t - 2
                if valid(u):
                    act.wait_ge(gneg_ready, u + 1)
                    a.activation(gexp[:, :], PS[:, O_BANK, GATE_AT:GATE_AT + E], ACT.Exp, bias=gneg[:, :],
                                 accum_out=gsum[:, :]).then_inc(gexp_ready, 1)
                u = t - 1
                if valid(u):
                    act.wait_ge(oT_ps, u + 1)
                    wait(act, wo_done, u)
                    a.activation(oT[:, :, :].rearrange("p k s -> p (k s)"), PS[:, T_BANK, 0:D],
                                 ACT.Copy).then_inc(oT_ready, 1)
                u = t + 1
                if valid(u):
                    for ps_ready, ready, dst, bank, c in ((q_ps, q_ready, qT, T_BANK, 0),
                                                          (k_ps, k_ready, kT, QK_BANK, 2)):
                        act.wait_ge(ps_ready, u + 1)
                        if not isinstance(u, int) or u >= 2:
                            act.wait_ge(st_done, RG * (u - 1))
                        a.activation(dst[1 - p][:, :, :].rearrange("p g s -> p (g s)"), PS[:, bank, :], ACT.Identity,
                                     scale=cols_sb[:, c:c + 1], bias=cols_sb[:, c + 1:c + 2]).then_inc(ready, 1)
                u = t + 2
                if valid(u):
                    act.wait_ge(aT_ps, u + 1)
                    wait(act, qkv_done, u)
                    a.activation(aT[:, :, :].rearrange("p k s -> p (k s)"), PS[:, T_BANK, 0:D],
                                 ACT.Copy).then_inc(aT_ready, 1)
            act.wait_ge(pool_const, 2)
            act.wait_ge(ld_small, 80)
            act.wait_ge(table_init, 32)
            attention(act, step)

            def x_out(t, p):
                act.wait_ge(xT_tr, t + 1)
                a.activation(xT_sb[p].rearrange("p k s -> p (k s)"), PS[:, T_BANK, 0:D], ACT.Copy).then_inc(xT_ready, 1)

            def silu(t, p):
                act.wait_ge(w13_done, t + 1)
                a.activation(h_sb[p].rearrange("p (c n) -> p c n", c=2), PS[:, 0:2, 0:FH],
                             ACT.Silu).then_inc(silu_ready, 1)

            def h_out(t, p):
                act.wait_ge(hT_tr, t + 1)
                a.activation(hT_sb[p][:, 0:4, :].rearrange("p k s -> p (k s)"), PS[:, 4, :],
                             ACT.Copy).then_inc(hT_a_ready, 1)

            def expert_step(t, p, j):
                silu(t, p)
                x_out(t + 1, 1 - p)
                h_out(t, p)
            x_out(0, 0)
            expert_step(0, 0, 0)
            experts(act, 1, 1, expert_step)

        @block.vector
        def _(dve):
            v = nc.vector
            k = [0]

            def plink(ins):
                k[0] += 1
                ins.then_inc(prep_step, 1)
                dve.wait_ge(prep_step, k[0])
            dve.wait_ge(ld_small, 80)
            v.tensor_copy(typesf[:, :], types_sb[:, :])
            v.tensor_tensor(pos_t0, pos_t0, rows_sb[:, 1, :], ALU.add)
            v.tensor_tensor(type_diff, type_diff, rows_sb[:, 1, :], ALU.subtract).then_inc(prep_done, 1)
            dve.wait_ge(ld_qkv, 48)
            for kk in range(DK):
                wqk = wqkv_sb[:, kk, 0:2 * D].rearrange("p (h s) -> p h s", s=HD)
                mean = prep[:, kk * 2 * H:(kk + 1) * 2 * H]
                plink(v.tensor_reduce(mean, wqk, axis=AX.X, op=ALU.add))
                plink(v.tensor_scalar(mean, mean, -1.0 / HD, None, ALU.mult))
                v.tensor_tensor(wqk, wqk, spread(mean, 2, HD),
                                ALU.add).then_inc(prep_done, 1)
            dve.wait_ge(pool_const, 2)

            def layernorm(link, src, c, eps, var, rs, t):
                link(v.bn_stats(st6[:, c, :], src))
                link(v.bn_aggr(mv[:, c, :], st6[:, c, :]))
                v.tensor_scalar(veps[:, c:c + 1], mv[:, c, 1:2], eps, None, ALU.add).then_inc(var, 1)
                dve.wait_ge(rs, t + 1)

            def step(t, p, j):
                link, clear = chain(dve, dve_chain)
                if valid(t):
                    for r in range(RG):
                        dve.wait_ge(s_done, RG * t + r + 1)
                        v.tensor_reduce(nmax[:, RG * r:RG * r + RG], PS[:, r, :].rearrange("p (g s) -> p g s", s=P),
                                        axis=AX.X, op=ALU.max, negate=True).then_inc(max_done, 1)
                    dve.wait_ge(max_done, RG * t + RG)
                    wait(dve, mT_tr, t)
                    link(v.tensor_copy(m3[:, 0, :], nmax[:, :]))
                    link(v.tensor_tensor(nres[:, :], nmax[:, :], m3[:, 0, :], ALU.subtract))
                    link(v.tensor_copy(m3[:, 1, :], nres[:, :]))
                    v.tensor_tensor(m3[:, 2, :], nres[:, :], m3[:, 1, :], ALU.subtract).then_inc(m3_ready, 1)
                u = t - 1
                if valid(u):
                    dve.wait_ge(pv_done, u + 1)
                    wait(dve, oT_ps, u)
                    po = PS[:, O_BANK, 0:H * VW].rearrange("p (h w) -> p h w", w=VW)
                    link(v.reciprocal(rden[:, :], po[:, :, HD]))
                    v.tensor_tensor(o_n[:, :].rearrange("p (h s) -> p h s", s=HD), po[:, :, 0:HD],
                                    spread(rden[:, :], 2, HD),
                                    ALU.mult).then_inc(o_ready, 1)
                if valid(t):
                    dve.wait_ge(mT_tr, t + 1)
                    v.tensor_copy(mT[:, :], mT_ps[0:3 * H, :]).then_inc(mT_ready, 1)
                u = t - 2
                if valid(u):
                    dve.wait_ge(gate_done, u + 1)
                    v.tensor_reduce(gneg[:, :], PS[:, O_BANK, GATE_AT:GATE_AT + E], axis=AX.X, op=ALU.max,
                                    negate=True).then_inc(gneg_ready, 1)
                    dve.wait_ge(gexp_ready, u + 1)
                    link(v.reciprocal(grs[:, :], gsum[:, :]))
                    link(v.tensor_scalar(score[:, :], gexp[:, :], grs[:, :], None, ALU.mult))
                    link(v.tensor_tensor(biased[:, :], score[:, :], ebias, ALU.add))
                    link(v.max(top8[:, :], biased[:, :]))
                    link(v.max_index(topi[:, :], top8[:, :], biased[:, :]))
                    link(v.tensor_copy(topf[:, :], topi[:, 0:TOPK]))
                    wait(dve, rank_done, u - 1)
                    link(v.tensor_scalar(oh0[:, :], iota_e[:, :], topf[:, 0:1], None, ALU.is_equal))
                    v.scalar_tensor_tensor(chosen[p][:, :], iota_e[:, :], topf[:, 1:2], oh0[:, :],
                                           ALU.is_equal, ALU.add).then_inc(chosen_ready, 1)
                    if not isinstance(u, int) or u >= 2:
                        dve.wait_ge(scattered[p], 16 * TOPK * half(j, p, -2))
                    for c in range(TOPK):
                        v.scalar_tensor_tensor(junk[:, c, :], iota_e[:, :], topf[:, c:c + 1], score[:, :],
                                               ALU.is_equal, ALU.mult, accum_out=entry[p][:, c, 1:2])
                    v.tensor_copy(entry[p][:, :, 0], dest_all[:, bass.ds(u, 1), :].rearrange("p o c -> p (o c)"))
                u = t + 1
                if valid(u):
                    dve.wait_ge(sq_ready, u + 1)
                    link(v.tensor_reduce(ss[:, :], sq[:, :].rearrange("p (h s) -> p h s", s=HD), axis=AX.X,
                                         op=ALU.add))
                    v.tensor_scalar(sse[:, :], ss[:, :], 1.0 / HD, 1e-5, ALU.mult, ALU.add).then_inc(var_qk, 1)
                    dve.wait_ge(rstd_qk, u + 1)
                    wait(dve, k_ps, u)
                    v.tensor_tensor(qkn[:, :, 0:HD], PS[:, QK_BANK, :].rearrange("p (h s) -> p h s", s=HD),
                                    spread(rqk[:, :], 2, HD),
                                    ALU.mult).then_inc(qkn_ready, 1)
                u = t + 3
                if valid(u):
                    q = 1 - p
                    x = x_in[q][:, :]
                    hu = h_all[:, bass.ds(u, 1), :].rearrange("p o d -> p (o d)")
                    dve.wait_ge(x_base_ready, u + 1)
                    dve.wait_ge(gathered[q], 16 * (half(j, p, 3) + 1))
                    v.tensor_tensor(x, x, x_base[:, :], ALU.add).then_inc(x_summed, 1)
                    dve.wait_ge(x_summed, u + 1)
                    layernorm(link, x, 0, 1e-12, var_e, rstd_e, u)
                    v.tensor_scalar(tmp[:, :], x, mv[:, 0, 0:1], rstd[:, 0:1], ALU.subtract, ALU.mult).then_inc(x_used, 1)
                    dve.wait_ge(x_used, u + 1)
                    link(v.tensor_tensor(tmp[:, :], tmp[:, :], gamma, ALU.mult))
                    link(v.tensor_tensor(hu, tmp[:, :], beta, ALU.add))
                    layernorm(link, hu, 1, 1e-5, var_a, rstd_a, u)
                    wait(dve, aT_ps, u - 1)
                    v.tensor_scalar(a_n[q][:, :], hu, mv[:, 1, 0:1], rstd[:, 1:2], ALU.subtract,
                                    ALU.mult).then_inc(a_ready, 1)
                u = t - 1
                if valid(u):
                    hu = h_all[:, bass.ds(u, 1), :].rearrange("p o d -> p (o d)")
                    dve.wait_ge(wo_done, u + 1)
                    dve.wait_ge(pool_bo, u + 1)
                    link(v.tensor_tensor(hu, hu, PS[:, VY_BANK, D:2 * D], ALU.add))
                    layernorm(link, hu, 2, 1e-5, var_f, rstd_f, u)
                    wait(dve, x2T_ps, u - 1)
                    if not isinstance(u, int) or u >= 2:
                        dve.wait_ge(x2_stored[1 - p], 16 * half(j, p, -1))
                    v.tensor_scalar(x2[1 - p][:, :], hu, mv[:, 2, 0:1], rstd[:, 2:3], ALU.subtract,
                                    ALU.mult).then_inc(x2_ready, 1)
                u = t - 2
                if valid(u):
                    dve.wait_ge(rank_done, u + 1)
                    v.tensor_tensor(chosen_sum[1 - p][:, :], chosen_sum[p][:, :], chosen[p][:, :],
                                    ALU.add).then_inc(sum_ready, 1)
                    link(v.tensor_tensor(ranked[:, :], PS[:, O_BANK, RANK_AT:RANK_AT + E], slot_base[:, :], ALU.add))
                    for c in range(TOPK):
                        last = v.scalar_tensor_tensor(junk[:, c, :], iota_e[:, :], topf[:, c:c + 1], ranked[:, :],
                                                      ALU.is_equal, ALU.mult, accum_out=slotf[p][:, c:c + 1])
                    last.then_inc(slot_ready, 1)
                clear()
            attention(dve, step)

            k[0] = 0

            def link(ins):
                k[0] += 1
                ins.then_inc(route_step, 1)
                dve.wait_ge(route_step, k[0])
            dve.wait_ge(counts_done, 1)
            counts = PS[:, O_BANK, RANK_AT:RANK_AT + E]
            link(v.tensor_tensor(over[:, :, :], spread(counts, 2, RB),
                                 spread(steps16[:, :], 1, E), ALU.is_gt))
            link(v.tensor_reduce(ntile[:, 0, :], over[:, :, :], axis=AX.X, op=ALU.add))
            for i, s in enumerate((1, 2, 4)):
                v.tensor_copy(ntile[:, i + 1, 0:s], ntile[:, i, 0:s])
                link(v.tensor_tensor(ntile[:, i + 1, s:E], ntile[:, i, s:E], ntile[:, i, 0:E - s], ALU.add))
            ends = ntile[:, 3, :]
            link(v.tensor_scalar(ended[:, 0, :], ends, tile_no[:, :], 0.0, ALU.is_le, ALU.add,
                                 accum_out=erow[:, 0:1]))
            link(v.tensor_tensor(ended[:, 1, :], ended[:, 0, :], ntile[:, 0, :], ALU.mult))
            link(v.tensor_reduce(erow[:, 1:2], ended[:, 1, :], axis=AX.X, op=ALU.add))
            link(v.tensor_tensor(erow[:, 2:3], tile_no[:, :], erow[:, 1:2], ALU.subtract))
            link(v.scalar_tensor_tensor(erow[:, 3:4], erow[:, 0:1], float(RB), erow[:, 2:3], ALU.mult, ALU.add))
            v.tensor_copy(rowi[:, :], erow[:, 3:4]).then_inc(rowi_ready, 1)
            link(v.tensor_tensor(le8[:, :, :], spread(ntile[0:1, 3, :], 1, NTP),
                                 spread(tile_row[:, :], 2, E), ALU.is_le))
            link(v.tensor_reduce(er[:, 0, :], le8[:, :, :], axis=AX.X, op=ALU.add))
            link(v.tensor_scalar(er[:, 1, :], er[:, 0, :], float(E - 1), None, ALU.min))
            v.tensor_copy(er_i[:, :], er[:, 1, :]).then_inc(er_ready, 1)
            dve.wait_ge(tab_tr, 1)
            v.tensor_copy(slot_score[:, :], PS[:, T_BANK, P:P + NTP])
            v.tensor_copy(dest_i[:, :], PS[:, T_BANK, 0:NTP])
            link(v.tensor_copy(dest[:, 0, :], PS[:, T_BANK, 0:NTP]))
            link(v.tensor_scalar(dest[:, 1, :], dest[:, 0, :], float(TOK), float(TOK), ALU.is_ge, ALU.mult))
            link(v.tensor_scalar(dest[:, 2, :], dest[:, 0, :], float(2 * TOK), float(TOK), ALU.is_ge, ALU.mult))
            link(v.tensor_tensor(dest[:, 0, :], dest[:, 0, :], dest[:, 1, :], ALU.subtract))
            link(v.tensor_tensor(dest[:, 0, :], dest[:, 0, :], dest[:, 2, :], ALU.subtract))
            v.tensor_copy(src_i[:, :], dest[:, 0, :]).then_inc(slots_ready, 1)

            def scale(t, p, n):
                dve.wait_ge(xg_loaded[p], 16 * n)
                v.tensor_scalar(xg_sb[p], xg_sb[p], slot_score[:, bass.ds(t, 1)], None, ALU.mult).then_inc(xs_ready, 1)

            def times(t, p):
                dve.wait_ge(silu_ready, t + 1)
                hp = h_sb[p].rearrange("p (c n) -> p c n", c=2)
                v.tensor_tensor(hp, hp, PS[:, 2:4, 0:FH], ALU.mult).then_inc(hh_ready, 1)

            def h_out(t, p):
                dve.wait_ge(hT_tr, t + 1)
                v.tensor_copy(hT_sb[p][:, 4, :], PS[:, 5, 0:P])
                v.tensor_copy(hT_sb[p][0:FT, 5, :], PS[0:FT, 5, P:2 * P]).then_inc(hT_v_ready, 1)

            def y_out(t, p, stored):
                dve.wait_ge(w2_done, t + 1)
                if stored is not None:
                    dve.wait_ge(y_stored[p], 16 * stored)
                v.tensor_copy(y_sb[p][:, :], PS[:, 7, 0:D]).then_inc(y_ready, 1)

            def expert_step(t, p, j):
                scale(t + 1, 1 - p, j + 2)
                times(t, p)
                y_out(t - 1, 1 - p, None if isinstance(t, int) and t <= 2 else j)
                h_out(t, p)
            scale(0, 0, 1)
            scale(1, 1, 1)
            times(0, 0)
            h_out(0, 0)
            experts(dve, 1, 3, expert_step)
            y_out(NT - 1, 0, NT // 2)

            for c in range(B // CH):
                dve.wait_ge(y_loaded[c], 32)
                hc = h_all[:, c * CH:(c + 1) * CH, :]
                v.tensor_tensor(hc, hc, y_back[c][:, 0, :, :], ALU.add).then_inc(sum_step, 1)
                dve.wait_ge(sum_step, c + 1)
                v.tensor_tensor(hc, hc, y_back[c][:, 1, :, :], ALU.add).then_inc(out_ready, 1)

        @block.tensor
        def _(pe):
            n = nc.tensor

            def bank_free(t, before, *others):
                for s, c in (before, *others) if isinstance(t, int) else (before,):
                    wait(pe, s, c)

            def transposes(src, count, width=P, rows=P, bank=T_BANK, at=0):
                for i in range(count):
                    last = n.transpose(PS[0:width, bank, at + i * rows:at + (i + 1) * rows],
                                       src[:, i * width:(i + 1) * width], ident[0:rows, 0:rows])
                return last

            def step(t, p, j):
                if valid(t):
                    pe.wait_ge(q_ready, t + 1)
                    pe.wait_ge(k_ready, t + 1)
                    for r in range(RG):
                        if not isinstance(t, int) or t > 0:
                            pe.wait_ge(exp_done, RG * (t - 1) + r + 1)
                        n.matmul(PS[:, r, :], identb[:, :],
                                 spread(mask_qk[:, :], 1, GROUPS),
                                 start=True, stop=True)
                    for g in range(GROUPS):
                        for r in range(RG):
                            rows = slice(HP * r, HP * r + HP)
                            last = n.matmul(PS[:, r, g * P:(g + 1) * P], qT[p][rows, g, :], kT[p][rows, g, :],
                                            start=False, stop=True, skip_group_check=True)
                            if g == GROUPS - 1:
                                last.then_inc(s_done, 1)
                u = t - 1
                if valid(u):
                    pe.wait_ge(exp_done, RG * u + RG)
                    pe.wait_ge(v_ready, u + 1)
                    wait(pe, slot_ready, u - 1)
                    if isinstance(u, int):
                        wait(pe, o_ready, u)
                    for h in range(H):
                        r, g = h % RG, h // RG
                        at = (r * GROUPS + g) * P
                        last = n.matmul(PS[:, O_BANK, h * VW:(h + 1) * VW], work[1 - p][:, at:at + P],
                                        v_aug[1 - p][:, h, :], start=True, stop=True)
                    last.then_inc(pv_done, 1)
                u = t + 1
                if valid(u):
                    pe.wait_ge(aT_ready, u + 1)
                    wait(pe, k_ready, u)
                    wait(pe, v_ready, u)
                    wait(pe, var_f, u - 2)
                    for bank, at, w0, w in ((QK_BANK, 0, 0, 2 * D), (VY_BANK, 0, 2 * D, D)):
                        for k in range(DK):
                            last = n.matmul(PS[:, bank, at:at + w], aT[:, k, :], wqkv_sb[:, k, w0:w0 + w],
                                            start=(k == 0), stop=(k == DK - 1))
                    last.then_inc(qkv_done, 1)
                if valid(t):
                    pe.wait_ge(m3_ready, t + 1)
                    wait(pe, o_ready, t)
                    n.transpose(mT_ps, m3[:, :, :].rearrange("p i c -> p (i c)"), identb[:, :]).then_inc(mT_tr, 1)
                u = t - 2
                if valid(u):
                    bank_free(t, (aT_ready, t + 2), (q_ready, t + 1), (oT_ready, t - 1), (x2T_ready, t - 2))
                    pe.wait_ge(x2_ready, u + 1)
                    transposes(x2[p], DK).then_inc(x2T_ps, 1)
                    pe.wait_ge(x2T_ready, u + 1)
                    wait(pe, mT_ready, t + 1)
                    if isinstance(t, int):
                        wait(pe, o_ready, t)
                        wait(pe, slot_ready, t - 2)
                    for k in range(DK):
                        last = n.matmul(PS[:, O_BANK, GATE_AT:GATE_AT + E], x2T[:, k, :], gate_sb[:, k, :],
                                        start=(k == 0), stop=(k == DK - 1))
                    last.then_inc(gate_done, 1)
                if valid(t):
                    pe.wait_ge(mT_ready, t + 1)
                    pe.wait_ge(max_done, RG * t + RG)
                    for r in range(RG):
                        n.matmul(PS[:, r, :], identb[:, :],
                                 spread(mask_kq[:, :], 1, GROUPS),
                                 start=True, stop=True)
                        for g in range(GROUPS):
                            n.matmul(PS[:, r, g * P:(g + 1) * P], sel[:, r * GROUPS + g, :], mT[:, :],
                                     start=False, stop=True, skip_group_check=True)
                    for g in range(GROUPS):
                        for r in range(RG):
                            rows = slice(HP * r, HP * r + HP)
                            last = n.matmul(PS[:, r, g * P:(g + 1) * P], kT[p][rows, g, :], qT[p][rows, g, :],
                                            start=False, stop=True, skip_group_check=True)
                            if g == GROUPS - 1:
                                last.then_inc(st_done, 1)
                u = t - 1
                if valid(u):
                    pe.wait_ge(o_ready, u + 1)
                    bank_free(t, (x2T_ready, t - 1), (aT_ready, t + 2), (q_ready, t + 1), (oT_ready, t - 1))
                    transposes(o_n, DK).then_inc(oT_ps, 1)
                u = t + 1
                if valid(u):
                    pe.wait_ge(qkn_ready, u + 1)
                    flat = qkn[:, :, :].rearrange("p h s -> p (h s)")
                    bank_free(t, (oT_ready, t), (x2T_ready, t - 1), (aT_ready, t + 2), (q_ready, t + 1))
                    transposes(flat[:, 0:H * HP], GROUPS).then_inc(q_ps, 1)
                    transposes(flat[:, H * HP:2 * H * HP], GROUPS, bank=QK_BANK).then_inc(k_ps, 1)
                u = t - 1
                if valid(u):
                    pe.wait_ge(oT_ready, u + 1)
                    wait(pe, var_f, u)
                    wait(pe, v_ready, t + 2)
                    for k in range(DK):
                        last = n.matmul(PS[:, VY_BANK, D:2 * D], oT[:, k, :], wo_sb[:, k, :],
                                        start=(k == 0), stop=(k == DK - 1))
                    last.then_inc(wo_done, 1)
                u = t + 2
                if valid(u):
                    pe.wait_ge(a_ready, u + 1)
                    bank_free(t, (q_ready, t + 2), (oT_ready, t), (x2T_ready, t - 1), (aT_ready, t + 2))
                    transposes(a_n[p], DK).then_inc(aT_ps, 1)
                u = t - 2
                if valid(u):
                    pe.wait_ge(chosen_ready, u + 1)
                    wait(pe, sum_ready, u)
                    pe.wait_ge(gexp_ready, u + 1)
                    ranks = PS[:, O_BANK, RANK_AT:RANK_AT + E]
                    n.matmul(ranks, upper[:, :], chosen[p][:, :], start=True, stop=False)
                    n.matmul(ranks, onesb[:, :], chosen_sum[p][:, :], start=False, stop=True).then_inc(rank_done, 1)

            pe.wait_ge(pool_const, 2)
            pe.wait_ge(prep_done, 1 + DK)
            attention(pe, step)

            pe.wait_ge(sum_ready, B)
            pe.wait_ge(slot_ready, B)
            n.matmul(PS[:, O_BANK, RANK_AT:RANK_AT + E], onesb[:, :], chosen_sum[0][:, :],
                     start=True, stop=True).then_inc(counts_done, 1)
            pe.wait_ge(trow_loaded, 16)
            for c in range(2):
                last = n.transpose(PS[:, T_BANK, c * P:c * P + NTP], trow[:, :, c], ident[0:NTP, 0:NTP])
            last.then_inc(tab_tr, 1)
            pe.wait_ge(er_ready, 1)
            pe.wait_ge(slots_ready, 1)
            pe.wait_ge(ld_ffn, 16 * 4 * E)

            def x_in_t(t, p):
                pe.wait_ge(xs_ready, t + 1)
                if not isinstance(t, int) or t > 0:
                    pe.wait_ge(xT_ready, t)
                transposes(xg_sb[p], DK).then_inc(xT_tr, 1)

            def up(t, p, e):
                pe.wait_ge(xT_ready, t + 1)
                if not isinstance(t, int) or t > 0:
                    pe.wait_ge(silu_ready, t)
                    pe.wait_ge(hh_ready, t)
                for c in range(4):
                    for k in range(DK):
                        last = n.matmul(PS[:, c, 0:FH], xT_sb[p][:, k, :],
                                        w13_sb[:, bass.ds(e, 1), k, c * FH:(c + 1) * FH],
                                        start=(k == 0), stop=(k == DK - 1))
                last.then_inc(w13_done, 1)

            def h_t(t, p):
                pe.wait_ge(hh_ready, t + 1)
                if not isinstance(t, int) or t > 0:
                    pe.wait_ge(hT_a_ready, t)
                    pe.wait_ge(hT_v_ready, t)
                for i in range(FK):
                    w = min(P, F - i * P)
                    last = n.transpose(PS[0:w, 4 + i // 4, i % 4 * P:(i % 4 + 1) * P],
                                       h_sb[p][:, i * P:i * P + w], ident[:, :])
                last.then_inc(hT_tr, 1)

            def down(t, p, e):
                pe.wait_ge(hT_a_ready, t + 1)
                pe.wait_ge(hT_v_ready, t + 1)
                if not isinstance(t, int) or t > 0:
                    pe.wait_ge(y_ready, t)
                for i in range(FK):
                    w = min(P, F - i * P)
                    last = n.matmul(PS[:, 7, 0:D], hT_sb[p][0:w, i, :], w2_sb[0:w, bass.ds(e, 1), i, :],
                                    start=(i == 0), stop=(i == FK - 1))
                last.then_inc(w2_done, 1)

            def expert_of(t):
                return pe.value_load(er_i[0:1, bass.ds(t, 1)], min_val=0, max_val=E - 1)

            def expert_step(t, p, j):
                up(t, p, expert_of(t))
                x_in_t(t + 1, 1 - p)
                down(t - 1, 1 - p, expert_of(t - 1))
                h_t(t, p)
            x_in_t(0, 0)
            up(0, 0, expert_of(0))
            x_in_t(1, 1)
            h_t(0, 0)
            experts(pe, 1, 3, expert_step)
            down(NT - 1, 0, expert_of(NT - 1))


def kernel(**inputs):
    import concourse.bacc as bacc
    import numpy as np
    from concourse.bass_utils import run_bass_kernel_spmd

    a = {name: np.asarray(v) for name, v in inputs.items()}

    def padded(v):
        return np.tile(np.concatenate([v, np.zeros(HP - HD, v.dtype)]), RG)

    bias_row = np.zeros(D, np.float32)
    bias_row[0:E] = a["L0_ffn_expert_bias"]
    arrays = {
        "ids": np.ascontiguousarray(a["x"].T),
        "types": np.ascontiguousarray(a["mask_BS_i1_0"].T),
        "word": a["L0_tok_word_emb"],
        "rows": np.concatenate([a["L0_tok_pos_emb"], a["L0_tok_type_emb"], a["L0_tok_gamma"][None],
                                a["L0_tok_beta"][None], a["L0_attn_bo"][None], bias_row[None]]),
        "w_qkv": np.concatenate([a["L0_attn_Wq"], a["L0_attn_Wk"], a["L0_attn_Wv"]], axis=1),
        "w_o": a["L0_attn_Wo"],
        "head_cols": np.stack([padded(a[f"L0_attn_{n}"]) for n in ("qln_w", "qln_b", "kln_w", "kln_b")], axis=1),
        "gate_t": np.ascontiguousarray(a["L0_ffn_gate_w"].T),
        "w1": a["L0_ffn_w1"],
        "w3": a["L0_ffn_w3"],
        "w2": a["L0_ffn_w2"],
    }
    arrays = {name: np.ascontiguousarray(v) for name, v in arrays.items()}
    nc = bacc.Bacc("TRN2", target_bir_lowering=False, num_devices=1)
    args = [nc.dram_tensor(f"{name}_dram", v.shape, mybir.dt.from_np(v.dtype), kind="ExternalInput").ap()
            for name, v in arrays.items()]
    out = nc.dram_tensor("out_dram", (B, P, D), mybir.dt.float32, kind="ExternalOutput").ap()
    build_tower(nc, *args, out)
    r = run_bass_kernel_spmd(nc, [{f"{name}_dram": v for name, v in arrays.items()}], core_ids=[0])
    return r.results[0]["out_dram"]
```

```python
from contextlib import ExitStack

import concourse.bass as bass
import concourse.mybir as mybir

P = 128
B = 16
D = 256
DK = D // P
H = 16
HD = D // H
HP = 32
GROUPS = H * HP // P
RG = P // HP
E = 8
F = 704
FH = F // 2
FK = -(-F // P)
FT = F - (FK - 1) * P
TOK = B * P
TOPK = 2
NT = (TOK * TOPK + E * (P - 1)) // P
NTP = NT + 2
RB = TOK // P
TROWS = E * RB + NTP - TOK * TOPK // P
NEG = -1.0e30
QK_BANK, VY_BANK, T_BANK, O_BANK = 4, 5, 6, 7
MT_AT, GATE_AT, RANK_AT = 256, 320, 288


def spread(ap, axis, count):
    ap = ap.unsqueeze(axis)
    shape = list(ap.shape)
    shape[axis] = count
    return ap.broadcast_to(shape)


def build_tower(nc, ids, types, word, rows, w_qkv, w_o, head_cols, gate_t, w1, w3, w2, out):
    f32, bf16, i32, u32 = mybir.dt.float32, mybir.dt.bfloat16, mybir.dt.int32, mybir.dt.uint32
    ALU, ACT, AX = mybir.AluOpType, mybir.ActivationFunctionType, mybir.AxisListType

    x2_dram = nc.dram_tensor("x2_rows", (TOK, D), f32).ap()
    table = nc.dram_tensor("slot_table", (TROWS * P, 2), f32).ap()

    ctx = ExitStack()
    with ctx:
        def sb(name, shape, dt=f32):
            return ctx.enter_context(nc.sbuf_tensor(name, shape, dt))

        def sem(name):
            return ctx.enter_context(nc.semaphore(name))

        w13_sb = sb("w13_sb", [P, E, DK, 2 * F])
        w2_sb = sb("w2_sb", [P, E, FK, D])
        h_all = sb("h_all", [P, B, D])
        wo_sb = sb("wo_sb", [P, DK, D])
        rows_sb = sb("rows_sb", [P, 6, D])
        ebias = sb("ebias", [P, E])
        gate_sb = sb("gate_sb", [P, DK, E])
        cols_sb = sb("cols_sb", [P, 4])
        ids_sb = sb("ids_sb", [P, B], i32)
        types_sb = sb("types_sb", [P, B], i32)
        typesf = sb("typesf", [P, B])
        ident = sb("ident", [P, P])
        identb = sb("identb", [P, P], bf16)
        upper = sb("upper", [P, P], bf16)
        onesb = sb("onesb", [P, P], bf16)
        mask_qk = sb("mask_qk", [P, P], bf16)
        mask_kq = sb("mask_kq", [P, P], bf16)
        sel = sb("sel", [P, H, P], bf16)
        neghalf = sb("neghalf", [P, 2 * H])
        iota_e = sb("iota_e", [P, E])
        slot_base = sb("slot_base", [P, E])
        dest_all = sb("dest_all", [P, B])
        idx = [sb(f"idx{p}", [P, 1], i32) for p in range(2)]
        tcol = sb("tcol", [P, 1])
        zeros = sb("zeros", [P, TOPK])
        x_in = [sb(f"x_in{p}", [P, D]) for p in range(2)]
        x_base = sb("x_base", [P, D])
        tmp = sb("tmp", [P, D])
        st6 = sb("st6", [P, 3, 6])
        mv = sb("mv", [P, 3, 2])
        veps = sb("veps", [P, 3])
        rstd = sb("rstd", [P, 3])
        a_n = [sb(f"a_n{p}", [P, D]) for p in range(2)]
        aT = sb("aT", [P, DK, P])
        v_aug = [sb(f"v_aug{p}", [P, H, HP]) for p in range(2)]
        o_raw = sb("o_raw", [P, GROUPS * P])
        ss = sb("ss", [P, 2 * H])
        sse = sb("sse", [P, 2 * H])
        rqk = sb("rqk", [P, 2 * H])
        qkn = sb("qkn", [P, 2 * H, HP])
        nmax = sb("nmax", [P, H])
        nres = sb("nres", [P, H])
        m3 = sb("m3", [P, P // H, H], bf16)
        mT = sb("mT", [P, P], bf16)
        work = [sb(f"work{p}", [P, 4 * 512]) for p in range(2)]
        rden = sb("rden", [P, H])
        oT = sb("oT", [P, DK, P])
        x2 = [sb(f"x2_{p}", [P, D]) for p in range(2)]
        x2T = sb("x2T", [P, DK, P])
        gneg = sb("gneg", [P, 1])
        gexp = sb("gexp", [P, E])
        gsum = sb("gsum", [P, 1])
        grs = sb("grs", [P, 1])
        score = sb("score", [P, E])
        biased = sb("biased", [P, E])
        top8 = sb("top8", [P, 8])
        topi = sb("topi", [P, 8], u32)
        topf = sb("topf", [P, TOPK])
        oh0 = sb("oh0", [P, E])
        junk = sb("junk", [P, 2, E])
        chosen = [sb(f"chosen{p}", [P, E], bf16) for p in range(2)]
        chosen_sum = [sb(f"chosen_sum{p}", [P, E], bf16) for p in range(2)]
        ranked = sb("ranked", [P, E])
        slotf = [sb(f"slotf{p}", [P, TOPK]) for p in range(2)]
        sloti = [sb(f"sloti{p}", [P, TOPK], i32) for p in range(2)]
        entry = [sb(f"entry{p}", [P, TOPK, 2]) for p in range(2)]
        steps16 = sb("steps16", [P, RB])
        ntile = sb("ntile", [P, 4, E])
        tile_no = sb("tile_no", [P, 1])
        tile_row = sb("tile_row", [1, NTP])
        ended = sb("ended", [P, 2, E])
        erow = sb("erow", [P, 4])
        rowi = sb("rowi", [P, 1], i32)
        er = sb("er", [1, 2, NTP])
        er_i = sb("er_i", [1, NTP], i32)
        dest = sb("dest", [P, 2, NTP])
        dest_i = sb("dest_i", [P, NTP], i32)
        src_i = sb("src_i", [P, NTP], i32)
        slot_score = sb("slot_score", [P, NTP])
        src_c = [sb(f"src_c{p}", [P, 1], i32) for p in range(2)]
        dst_c = [sb(f"dst_c{p}", [P, 1], i32) for p in range(2)]
        PS = ctx.enter_context(nc.psum_tensor("PS", [P, 8, 512], f32))

        wqkv_sb = w2_sb[:, E - 1, :, :].rearrange("p k d -> p (k d)").rearrange("p (k n) -> p k n", k=DK)
        prep = o_raw[:, 0:2 * DK * H]
        late = w13_sb[:, E - 1, :, :].rearrange("p k n -> p (k n)")
        qT, kT = ([late[:, (2 * i + p) * 512:(2 * i + p + 1) * 512].rearrange("p (g s) -> p g s", s=P)
                   for p in range(2)] for i in range(2))
        sq = late[:, 2048:2560]
        o_n = rows_sb[:, 1, :]
        over = work[1][:, 0:E * RB].rearrange("p (e j) -> p e j", e=E)
        le8 = work[1][0:1, 128:128 + NTP * E].rearrange("p (t e) -> p t e", e=E)
        trow = work[1][0:NTP, 512:512 + 2 * P].rearrange("p (s c) -> p s c", c=2)

        pos_t0, type_diff = rows_sb[:, 0, :], rows_sb[:, 2, :]
        gamma, beta, bo = rows_sb[:, 3, :], rows_sb[:, 4, :], rows_sb[:, 5, :]
        part_of = work[1][:, D:D + H]
        mT_ps = PS[:, T_BANK, MT_AT:MT_AT + P // 2].bitcast(bf16)
        init_rows = work[0][:, 0:2 * P].rearrange("p (s c) -> p s c", c=2)
        zero_rows = work[1][:, 0:D]

        def part(p, at, n):
            return work[p][:, at:at + n]
        XG, XT, HH, HT = 0, 256, 512, 512 + F
        hT_sb = [part(p, HT, FK * P).rearrange("p (k s) -> p k s", k=FK) for p in range(2)]
        h_sb = [part(p, HH, F) for p in range(2)]
        xg_sb = [part(p, XG, D) for p in range(2)]
        xT_sb = [part(p, XT, D).rearrange("p (k s) -> p k s", k=DK) for p in range(2)]
        y_sb = x_in

        ld_ids, ld_small, ld_qkv, ld_ffn = sem("ld_ids"), sem("ld_small"), sem("ld_qkv"), sem("ld_ffn")
        pool_const, pool_step = sem("pool_const"), sem("pool_step")
        prep_done, prep_step = sem("prep_done"), sem("prep_step")
        table_init = sem("table_init")
        gathered = [sem(f"gathered{p}") for p in range(2)]
        pool_chain, dve_chain = sem("pool_chain"), sem("dve_chain")
        x_base_ready, x_summed, pool_bo = sem("x_base_ready"), sem("x_summed"), sem("pool_bo")
        var_e, var_a, var_f, var_qk = sem("var_e"), sem("var_a"), sem("var_f"), sem("var_qk")
        rstd_e, rstd_a, rstd_f, rstd_qk = sem("rstd_e"), sem("rstd_a"), sem("rstd_f"), sem("rstd_qk")
        x_used, a_ready = sem("x_used"), sem("a_ready")
        m3_ready, chosen_ready, slot_ready = sem("m3_ready"), sem("chosen_ready"), sem("slot_ready")
        aT_ps, aT_ready, qk_done, v_done, v_ready, sq_ready = (
            sem("aT_ps"), sem("aT_ready"), sem("qk_done"), sem("v_done"), sem("v_ready"), sem("sq_ready"))
        qkn_ready, q_ps, k_ps, q_ready, k_ready = (
            sem("qkn_ready"), sem("q_ps"), sem("k_ps"), sem("q_ready"), sem("k_ready"))
        s_done, max_done, mT_tr, mT_ready = (
            sem("s_done"), sem("max_done"), sem("mT_tr"), sem("mT_ready"))
        st_done, exp_done, pv_done, o_ready = sem("st_done"), sem("exp_done"), sem("pv_done"), sem("o_ready")
        o_raw_ready, o_back = sem("o_raw_ready"), sem("o_back")
        oT_ps, oT_ready, wo_done = sem("oT_ps"), sem("oT_ready"), sem("wo_done")
        x2_ready, x2T_ps, x2T_ready = sem("x2_ready"), sem("x2T_ps"), sem("x2T_ready")
        x2_stored = [sem(f"x2_stored{p}") for p in range(2)]
        gate_done, gneg_ready, gexp_ready = sem("gate_done"), sem("gneg_ready"), sem("gexp_ready")
        rank_done, sum_ready = sem("rank_done"), sem("sum_ready")
        scattered = [sem(f"scattered{p}") for p in range(2)]
        counts_done, rowi_ready, route_step, er_ready = (
            sem("counts_done"), sem("rowi_ready"), sem("route_step"), sem("er_ready"))
        trow_loaded, tab_tr, slots_ready = sem("trow_loaded"), sem("tab_tr"), sem("slots_ready")
        xg_loaded = [sem(f"xg_loaded{p}") for p in range(2)]
        xs_ready, xT_tr, xT_ready = sem("xs_ready"), sem("xT_tr"), sem("xT_ready")
        w13_done, silu_ready, hh_ready = sem("w13_done"), sem("silu_ready"), sem("hh_ready")
        hT_tr, hT_a_ready, hT_v_ready = sem("hT_tr"), sem("hT_a_ready"), sem("hT_v_ready")
        w2_done, y_ready = sem("w2_done"), sem("y_ready")
        y_stored = [sem(f"y_stored{p}") for p in range(2)]
        h_stored = sem("h_stored")

        block = ctx.enter_context(nc.Block())

        def wait(eng, s, n):
            if isinstance(n, int):
                n = min(n, B)
                if n <= 0:
                    return
            eng.wait_ge(s, n)

        def chain(eng, s):
            k = [0]

            def link(ins):
                k[0] += 1
                ins.then_inc(s, 1)
                eng.wait_ge(s, k[0])

            def clear():
                eng.sem_clear(s)
            return link, clear

        AHEAD, BEHIND = 4, 3
        LOOP = 4

        def valid(t):
            return not isinstance(t, int) or 0 <= t < B

        def half(j, p, ahead):
            return j + (p + ahead) // 2

        def attention(eng, step):
            for t in range(-AHEAD, LOOP):
                step(t, t % 2, t // 2)
            with eng.Fori(LOOP // 2, (B - AHEAD) // 2) as j:
                for p in range(2):
                    step(2 * j + p, p, j)
            for t in range(B - AHEAD, B + BEHIND):
                step(t, t % 2, t // 2)

        def experts(eng, first, loop_first, step):
            for t in range(first, loop_first):
                step(t, t % 2, (t - 1) // 2)
            with eng.Fori((loop_first - 1) // 2, (NT - 1) // 2) as j:
                for i in range(2):
                    step(2 * j + 1 + i, 1 - i, j)

        @block.sync
        def _(sp):
            sp.dma_start(ids_sb[:, :], ids).then_inc(ld_ids, 16)
            sp.dma_start(types_sb[:, :], types).then_inc(ld_small, 16)
            sp.dma_start(rows_sb[:, 0, :], rows[0:P, :]).then_inc(ld_small, 16)
            sp.dma_start(rows_sb[:, 1:6, :],
                         spread(rows[P:P + 5, :], 0, P)).then_inc(ld_small, 16)
            sp.dma_start(ebias[:, :], spread(rows[P + 5, 0:E], 0, P)).then_inc(ld_small, 16)
            sp.dma_start(cols_sb[:, :], head_cols).then_inc(ld_small, 16)
            sp.dma_start(wqkv_sb[:, :, :], w_qkv.rearrange("(k p) n -> p k n", p=P)).then_inc(ld_qkv, 16)
            sp.dma_start(wo_sb[:, :, :], w_o.rearrange("(k p) n -> p k n", p=P)).then_inc(ld_qkv, 16)
            sp.dma_start(gate_sb[:, :, :], gate_t.rearrange("(k p) n -> p k n", p=P)).then_inc(ld_qkv, 16)
            sp.wait_ge(pool_const, 1)
            sp.dma_start(table[0:P * P, :].rearrange("(r s) c -> r (s c)", s=P),
                         init_rows.rearrange("p s c -> p (s c)")).then_inc(table_init, 16)
            sp.dma_start(table[P * P:TROWS * P, :].rearrange("(r s) c -> r (s c)", s=P),
                         init_rows[0:TROWS - P].rearrange("p s c -> p (s c)")).then_inc(table_init, 16)
            sp.dma_start(out[TOK:TOK + P, :], zero_rows).then_inc(table_init, 16)

            def load_expert(e):
                sp.dma_start(w13_sb[:, e, :, 0:F], w1[e].rearrange("(k p) n -> p k n", p=P)).then_inc(ld_ffn, 16)
                sp.dma_start(w13_sb[:, e, :, F:2 * F], w3[e].rearrange("(k p) n -> p k n", p=P)).then_inc(ld_ffn, 16)
                sp.dma_start(w2_sb[:, e, 0:FK - 1, :],
                             w2[e, 0:F - FT].rearrange("(k p) n -> p k n", p=P)).then_inc(ld_ffn, 16)
                sp.dma_start(w2_sb[0:FT, e, FK - 1, :], w2[e, F - FT:F]).then_inc(ld_ffn, 16)

            def step(t, p, j):
                u = t - 2
                if valid(u):
                    sp.wait_ge(x2_ready, u + 1)
                    sp.dma_start(x2_dram[bass.ds(u * P, P), :], x2[p][:, :]).then_inc(x2_stored[p], 16)
                    sp.dma_start(out[bass.ds(u * P, P), :],
                                 h_all[:, bass.ds(u, 1), :].rearrange("p o d -> p (o d)")).then_inc(h_stored, 16)
                if isinstance(t, int) and 0 <= t < LOOP:
                    sp.wait_ge(x_summed, t + AHEAD)
                    for e in range(2 * t, min(2 * t + 2, E - 1)):
                        load_expert(e)
            attention(sp, step)

            sp.wait_ge(v_done, B)
            sp.wait_ge(var_qk, B)
            sp.wait_ge(st_done, RG * B)
            load_expert(E - 1)

        @block.gpsimd
        def _(pool):
            g = nc.gpsimd
            k = [0]

            def link(ins):
                k[0] += 1
                ins.then_inc(pool_step, 1)
                pool.wait_ge(pool_step, k[0])
            g.memset(zero_rows, 0.0)
            link(g.memset(init_rows, 0.0))
            g.memset(neghalf[:, :], -0.5)
            g.iota(init_rows[:, :, 0], pattern=[[1, P]], base=TOK, channel_multiplier=0,
                   allow_small_or_imprecise_dtypes=True).then_inc(pool_const, 1)

            def constants_1():
                link(g.memset(ident[:, :], 0.0))
                link(g.affine_select(out=ident[:, :], in_=ident[:, :], compare_op=ALU.not_equal, fill=1.0,
                                     base=0, pattern=[[-1, P]], channel_multiplier=1))
                g.tensor_copy(identb[:, :], ident[:, :])
                for p in range(2):
                    g.memset(v_aug[p][:, :, HD:HP], 1.0)
                g.memset(m3[:, :, :], 0.0)
                g.memset(qkn[:, :, :], 0.0).then_inc(pool_const, 1)

            def constants_2():
                g.memset(mask_qk[:, :], 0.0)
                g.memset(mask_kq[:, :], 0.0)
                link(g.memset(onesb[:, :], 1.0))
                g.affine_select(out=mask_qk[:, :], in_=mask_qk[:, :], compare_op=ALU.is_ge, fill=NEG,
                                base=0, pattern=[[-1, P]], channel_multiplier=1)
                g.affine_select(out=mask_kq[:, :], in_=mask_kq[:, :], compare_op=ALU.is_ge, fill=NEG,
                                base=0, pattern=[[1, P]], channel_multiplier=-1)
                g.affine_select(out=upper[:, :], in_=onesb[:, :], compare_op=ALU.is_gt, fill=0.0,
                                base=0, pattern=[[1, P]], channel_multiplier=-1)
                exact = dict(allow_small_or_imprecise_dtypes=True)
                g.iota(iota_e[:, :], pattern=[[1, E]], base=0, channel_multiplier=0, **exact)
                g.iota(slot_base[:, :], pattern=[[TOK, E]], base=0, channel_multiplier=0, **exact)
                g.iota(dest_all[:, :], pattern=[[P, B]], base=0, channel_multiplier=1, **exact)
                g.iota(steps16[:, :], pattern=[[P, RB]], base=0, channel_multiplier=0, **exact)
                g.iota(tile_no[:, :], pattern=[[0, 1]], base=0, channel_multiplier=1, **exact)
                g.iota(tile_row[:, :], pattern=[[1, NTP]], base=0, channel_multiplier=0, **exact)
                g.memset(chosen_sum[0][:, :], 0.0)
                g.memset(zeros[:, :], 0.0)
                link(g.memset(part_of[:, :], 0.0))
                for i in range(3):
                    last = g.affine_select(out=part_of[:, :], in_=part_of[:, :], compare_op=ALU.not_equal, fill=1.0,
                                           base=-i * H, pattern=[[-1, H]], channel_multiplier=1)
                    if i < 2:
                        link(last)
                last.then_inc(pool_const, 1)
            pool.wait_ge(ld_ids, 16)

            def qk_power(u):
                pool.wait_ge(var_qk, u + 1)
                g.tensor_tensor(rqk[:, :], sse[:, :], neghalf[:, :], ALU.pow).then_inc(rstd_qk, 1)

            def step(t, p, j):
                link, clear = chain(pool, pool_chain)
                u = t + 3
                if isinstance(t, int) and t == 1 - AHEAD:
                    pool.wait_ge(prep_done, 1)
                if valid(u):
                    q = 1 - p
                    wait(pool, x_summed, u)
                    link(g.tensor_copy(tcol[:, :], typesf[:, bass.ds(u, 1)]))
                    link(g.tensor_scalar(x_base[:, :], type_diff, tcol[:, :], None, ALU.mult))
                    g.tensor_tensor(x_base[:, :], x_base[:, :], pos_t0, ALU.add).then_inc(x_base_ready, 1)
                early = isinstance(t, int) and t == -1
                if early:
                    qk_power(t + 1)
                u = t - 2
                if valid(u):
                    pool.wait_ge(var_f, u + 1)
                    g.tensor_tensor(rstd[:, 2:3], veps[:, 2:3], neghalf[:, 0:1], ALU.pow).then_inc(rstd_f, 1)
                u = t + 3
                if valid(u):
                    pool.wait_ge(var_e, u + 1)
                    g.tensor_tensor(rstd[:, 0:1], veps[:, 0:1], neghalf[:, 0:1], ALU.pow).then_inc(rstd_e, 1)
                u = t + 4
                if valid(u):
                    wait(pool, x_used, u - 1)
                    link(g.tensor_copy(idx[p][:, :], ids_sb[:, bass.ds(u, 1)]))
                    g.indirect_dma_start(x_in[p][:, :], None, word,
                                         bass.IndirectOffsetOnAxis(idx[p][:, :], 0)).then_inc(gathered[p], 16)
                u = t - 3
                if valid(u):
                    q = 1 - p
                    if isinstance(u, int) and u == 0:
                        pool.wait_ge(table_init, 48)
                    pool.wait_ge(slot_ready, u + 1)
                    link(g.tensor_tensor(slotf[q][:, :], slotf[q][:, :], zeros[:, :], ALU.add))
                    link(g.tensor_copy(sloti[q][:, :], slotf[q][:, :]))
                    for c in range(TOPK):
                        g.indirect_dma_start(table, bass.IndirectOffsetOnAxis(sloti[q][:, c:c + 1], 0),
                                             entry[q][:, c, :], None).then_inc(scattered[q], 16)
                if valid(t + 1) and not early:
                    qk_power(t + 1)
                u = t + 3
                if valid(u):
                    pool.wait_ge(var_a, u + 1)
                    g.tensor_tensor(rstd[:, 1:2], veps[:, 1:2], neghalf[:, 0:1], ALU.pow).then_inc(rstd_a, 1)
                    pool.wait_ge(a_ready, u + 1)
                    hu = h_all[:, bass.ds(u, 1), :].rearrange("p o d -> p (o d)")
                    g.tensor_tensor(hu, hu, bo, ALU.add).then_inc(pool_bo, 1)
                clear()
                if isinstance(t, int) and t == -AHEAD:
                    constants_1()
                if isinstance(t, int) and t == 1 - AHEAD:
                    constants_2()

            attention(pool, step)

            for p in range(2):
                pool.wait_ge(scattered[p], 16 * TOPK * B // 2)
            pool.wait_ge(rowi_ready, 1)
            g.indirect_dma_start(trow[:, :, :].rearrange("t s c -> t (s c)"), None,
                                 table.rearrange("(r s) c -> r (s c)", s=P),
                                 bass.IndirectOffsetOnAxis(rowi[0:NTP, :], 0)).then_inc(trow_loaded, 16)
            pool.wait_ge(slots_ready, 1)
            for p in range(2):
                pool.wait_ge(x2_stored[p], 16 * B // 2)
            pool.wait_ge(h_stored, 16 * B)

            def gather(t, p, link):
                link(g.tensor_copy(src_c[p][:, :], src_i[:, bass.ds(t, 1)]))
                g.indirect_dma_start(xg_sb[p], None, x2_dram,
                                     bass.IndirectOffsetOnAxis(src_c[p][:, :], 0)).then_inc(xg_loaded[p], 16)

            def scatter(t, p, link):
                pool.wait_ge(y_ready, t + 1)
                link(g.tensor_copy(dst_c[p][:, :], dest_i[:, bass.ds(t, 1)]))
                g.indirect_dma_start(out, bass.IndirectOffsetOnAxis(dst_c[p][:, :], 0), y_sb[p][:, :],
                                     None, compute_op=ALU.add).then_inc(y_stored[p], 16)

            def step(t, p, j):
                link, clear = chain(pool, pool_chain)
                pool.wait_ge(xT_tr, t + 1)
                pool.wait_ge(xg_loaded[p], 16 * (j + 2 - p))
                gather(t + 2, p, link)
                if not isinstance(t, int) or t > 2:
                    pool.wait_ge(y_stored[1 - p], 16 * j)
                if not isinstance(t, int) or t > 1:
                    pool.wait_ge(y_stored[p], 16 * (j + 1 - p))
                scatter(t - 1, 1 - p, link)
                clear()
            link, clear = chain(pool, pool_chain)
            gather(0, 0, link)
            gather(1, 1, link)
            pool.wait_ge(xT_tr, 1)
            pool.wait_ge(xg_loaded[0], 16)
            gather(2, 0, link)
            clear()
            experts(pool, 1, 3, step)
            for p in range(2):
                pool.wait_ge(y_stored[p], 16 * (NT // 2))
            scatter(NT - 1, 0, chain(pool, pool_chain)[0])
            pool.wait_ge(y_stored[0], 16 * (NT - NT // 2))

        @block.scalar
        def _(act):
            a = nc.scalar

            def step(t, p, j):
                u = t + 1
                if valid(u):
                    act.wait_ge(qk_done, u + 1)
                    wait(act, var_qk, u)
                    a.activation(sq[:, :], PS[:, QK_BANK, :], ACT.Square).then_inc(sq_ready, 1)
                u = t - 2
                if valid(u):
                    act.wait_ge(x2T_ps, u + 1)
                    wait(act, gate_done, u)
                    a.activation(x2T[:, :, :].rearrange("p k s -> p (k s)"), PS[:, T_BANK, 0:D],
                                 ACT.Copy).then_inc(x2T_ready, 1)
                u = t - 1
                if valid(u):
                    act.wait_ge(pv_done, u + 1)
                    wait(act, o_back, u)
                    a.activation(o_raw[:, :], PS[:, O_BANK, :], ACT.Copy).then_inc(o_raw_ready, 1)
                u = t - 2
                if valid(u):
                    act.wait_ge(gneg_ready, u + 1)
                    a.activation(gexp[:, :], PS[:, T_BANK, GATE_AT:GATE_AT + E], ACT.Exp, bias=gneg[:, :],
                                 accum_out=gsum[:, :]).then_inc(gexp_ready, 1)
                u = t + 1
                if valid(u):
                    act.wait_ge(v_done, u + 1)
                    wait(act, pv_done, u - 1)
                    a.activation(v_aug[1 - p][:, :, 0:HD], PS[:, VY_BANK, 0:D].rearrange("p (h s) -> p h s", s=HD),
                                 ACT.Copy).then_inc(v_ready, 1)

                def probabilities(banks):
                    for r in banks:
                        act.wait_ge(st_done, RG * t + r + 1)
                        a.activation(work[p][:, r * 512:(r + 1) * 512], PS[:, r, :], ACT.Exp,
                                     scale=HD ** -0.5).then_inc(exp_done, 1)
                if valid(t):
                    if isinstance(t, int) and t == 1:
                        act.wait_ge(prep_done, 2 + DK)
                    wait(act, pv_done, t - 1)
                    probabilities(range(0, 2))
                u = t - 1
                if valid(u):
                    act.wait_ge(oT_ps, u + 1)
                    wait(act, wo_done, u)
                    a.activation(oT[:, :, :].rearrange("p k s -> p (k s)"), PS[:, O_BANK, 0:D],
                                 ACT.Copy).then_inc(oT_ready, 1)
                u = t + 1
                if valid(u):
                    act.wait_ge(q_ps, u + 1)
                    if not isinstance(u, int) or u >= 2:
                        act.wait_ge(st_done, RG * (u - 1))
                    a.activation(qT[1 - p][:, :, :].rearrange("p g s -> p (g s)"), PS[:, T_BANK, :], ACT.Identity,
                                 scale=cols_sb[:, 0:1], bias=cols_sb[:, 1:2]).then_inc(q_ready, 1)
                if valid(t):
                    probabilities(range(2, RG))
                u = t + 2
                if valid(u):
                    act.wait_ge(aT_ps, u + 1)
                    wait(act, v_done, u)
                    a.activation(aT[:, :, :].rearrange("p k s -> p (k s)"), PS[:, O_BANK, 0:D],
                                 ACT.Copy).then_inc(aT_ready, 1)
            act.wait_ge(pool_const, 1)
            a.activation(gneg[:, :], neghalf[:, 0:1], ACT.Exp)
            act.wait_ge(pool_const, 2)
            act.wait_ge(ld_small, 80)
            act.wait_ge(table_init, 48)
            attention(act, step)

            def x_out(t, p):
                act.wait_ge(xT_tr, t + 1)
                a.activation(xT_sb[p].rearrange("p k s -> p (k s)"), PS[:, T_BANK, 0:D], ACT.Copy).then_inc(xT_ready, 1)

            def silu(t, p):
                act.wait_ge(w13_done, t + 1)
                a.activation(h_sb[p].rearrange("p (c n) -> p c n", c=2), PS[:, 0:2, 0:FH],
                             ACT.Silu).then_inc(silu_ready, 1)

            def h_out(t, p):
                act.wait_ge(hT_tr, t + 1)
                a.activation(hT_sb[p][:, 0:4, :].rearrange("p k s -> p (k s)"), PS[:, 4, :],
                             ACT.Copy).then_inc(hT_a_ready, 1)

            def expert_step(t, p, j):
                silu(t, p)
                x_out(t + 1, 1 - p)
                h_out(t, p)
            x_out(0, 0)
            expert_step(0, 0, 0)
            experts(act, 1, 1, expert_step)

        @block.vector
        def _(dve):
            v = nc.vector
            k = [0]

            def plink(ins):
                k[0] += 1
                ins.then_inc(prep_step, 1)
                dve.wait_ge(prep_step, k[0])
            dve.wait_ge(ld_small, 80)
            v.tensor_copy(typesf[:, :], types_sb[:, :])
            v.tensor_tensor(pos_t0, pos_t0, rows_sb[:, 1, :], ALU.add)
            v.tensor_tensor(type_diff, type_diff, rows_sb[:, 1, :], ALU.subtract).then_inc(prep_done, 1)
            def center_weights():
                dve.wait_ge(ld_qkv, 48)
                for kk in range(DK):
                    wqk = wqkv_sb[:, kk, 0:2 * D].rearrange("p (h s) -> p h s", s=HD)
                    mean = prep[:, kk * 2 * H:(kk + 1) * 2 * H]
                    plink(v.tensor_reduce(mean, wqk, axis=AX.X, op=ALU.add))
                    plink(v.tensor_scalar(mean, mean, -1.0 / HD, None, ALU.mult))
                    v.tensor_tensor(wqk, wqk, spread(mean, 2, HD),
                                    ALU.add).then_inc(prep_done, 1)
            dve.wait_ge(pool_const, 2)

            def stats(link, src, c, eps, var):
                link(v.bn_stats(st6[:, c, :], src))
                link(v.bn_aggr(mv[:, c, :], st6[:, c, :]))
                v.tensor_scalar(veps[:, c:c + 1], mv[:, c, 1:2], eps, None, ALU.add).then_inc(var, 1)

            def normalize(dst, src, c):
                return v.tensor_scalar(dst, src, mv[:, c, 0:1], rstd[:, c:c + 1], ALU.subtract, ALU.mult)

            def qk_variance(u, link):
                dve.wait_ge(sq_ready, u + 1)
                link(v.tensor_reduce(ss[:, :], sq[:, :].rearrange("p (h s) -> p h s", s=HD), axis=AX.X,
                                     op=ALU.add))
                v.tensor_scalar(sse[:, :], ss[:, :], 1.0 / HD, 1e-5, ALU.mult, ALU.add).then_inc(var_qk, 1)

            def row(u):
                return h_all[:, bass.ds(u, 1), :].rearrange("p o d -> p (o d)")

            def step(t, p, j):
                link, clear = chain(dve, dve_chain)
                q = 1 - p
                if isinstance(t, int) and t == -2:
                    center_weights()
                    dve.wait_ge(pool_const, 3)
                    v.tensor_copy(sel[:, :, :], spread(part_of, 2, P)).then_inc(prep_done, 1)
                early = isinstance(t, int) and t == -1
                if early:
                    qk_variance(t + 1, link)
                u = t - 2
                if valid(u):
                    dve.wait_ge(wo_done, u + 1)
                    dve.wait_ge(pool_bo, u + 1)
                    link(v.tensor_tensor(row(u), row(u), PS[:, VY_BANK, D:2 * D], ALU.add))
                    stats(link, row(u), 2, 1e-5, var_f)
                u = t + 3
                if valid(u):
                    x = x_in[q][:, :]
                    dve.wait_ge(x_base_ready, u + 1)
                    dve.wait_ge(gathered[q], 16 * (half(j, p, 3) + 1))
                    v.tensor_tensor(x, x, x_base[:, :], ALU.add).then_inc(x_summed, 1)
                    dve.wait_ge(x_summed, u + 1)
                    stats(link, x, 0, 1e-12, var_e)
                u = t - 2
                if valid(u):
                    dve.wait_ge(rstd_f, u + 1)
                    wait(dve, x2T_ps, u - 1)
                    if not isinstance(u, int) or u >= 2:
                        dve.wait_ge(x2_stored[p], 16 * half(j, p, -2))
                    normalize(x2[p][:, :], row(u), 2).then_inc(x2_ready, 1)
                u = t - 3
                if valid(u):
                    dve.wait_ge(rank_done, u + 1)
                    wait(dve, aT_ready, t + 2)
                    v.tensor_tensor(chosen_sum[p][:, :], chosen_sum[q][:, :], chosen[q][:, :],
                                    ALU.add).then_inc(sum_ready, 1)
                    link(v.tensor_tensor(ranked[:, :], PS[:, O_BANK, RANK_AT:RANK_AT + E], slot_base[:, :], ALU.add))
                    for c in range(TOPK):
                        last = v.scalar_tensor_tensor(junk[:, c, :], iota_e[:, :], topf[:, c:c + 1], ranked[:, :],
                                                      ALU.is_equal, ALU.mult, accum_out=slotf[q][:, c:c + 1])
                    last.then_inc(slot_ready, 1)
                if valid(t):
                    for r in range(RG):
                        dve.wait_ge(s_done, RG * t + r + 1)
                        v.tensor_reduce(nmax[:, RG * r:RG * r + RG], PS[:, r, :].rearrange("p (g s) -> p g s", s=P),
                                        axis=AX.X, op=ALU.max, negate=True).then_inc(max_done, 1)
                    dve.wait_ge(max_done, RG * t + RG)
                    wait(dve, mT_tr, t)
                    link(v.tensor_copy(m3[:, 0, :], nmax[:, :]))
                    link(v.tensor_tensor(nres[:, :], nmax[:, :], m3[:, 0, :], ALU.subtract))
                    link(v.tensor_copy(m3[:, 1, :], nres[:, :]))
                    v.tensor_tensor(m3[:, 2, :], nres[:, :], m3[:, 1, :], ALU.subtract).then_inc(m3_ready, 1)
                if valid(t + 1) and not early:
                    qk_variance(t + 1, link)
                u = t - 2
                if valid(t):
                    dve.wait_ge(mT_tr, t + 1)
                    if valid(u):
                        dve.wait_ge(gate_done, u + 1)
                    v.tensor_copy(mT[:, :], mT_ps).then_inc(mT_ready, 1)
                if valid(u):
                    dve.wait_ge(gate_done, u + 1)
                    v.tensor_reduce(gneg[:, :], PS[:, T_BANK, GATE_AT:GATE_AT + E], axis=AX.X, op=ALU.max,
                                    negate=True).then_inc(gneg_ready, 1)
                u = t + 3
                if valid(u):
                    dve.wait_ge(rstd_e, u + 1)
                    normalize(tmp[:, :], x_in[q][:, :], 0).then_inc(x_used, 1)
                    dve.wait_ge(x_used, u + 1)
                    link(v.tensor_tensor(tmp[:, :], tmp[:, :], gamma, ALU.mult))
                    link(v.tensor_tensor(row(u), tmp[:, :], beta, ALU.add))
                    stats(link, row(u), 1, 1e-5, var_a)
                u = t - 2
                if valid(u):
                    dve.wait_ge(gexp_ready, u + 1)
                    link(v.reciprocal(grs[:, :], gsum[:, :]))
                    link(v.tensor_scalar(score[:, :], gexp[:, :], grs[:, :], None, ALU.mult))
                    link(v.tensor_tensor(biased[:, :], score[:, :], ebias[:, :], ALU.add))
                    link(v.max(top8[:, :], biased[:, :]))
                    link(v.max_index(topi[:, :], top8[:, :], biased[:, :]))
                    link(v.tensor_copy(topf[:, :], topi[:, 0:TOPK]))
                    wait(dve, rank_done, u - 1)
                    link(v.tensor_scalar(oh0[:, :], iota_e[:, :], topf[:, 0:1], None, ALU.is_equal))
                    v.scalar_tensor_tensor(chosen[p][:, :], iota_e[:, :], topf[:, 1:2], oh0[:, :],
                                           ALU.is_equal, ALU.add).then_inc(chosen_ready, 1)
                    if not isinstance(u, int) or u >= 2:
                        dve.wait_ge(scattered[p], 16 * TOPK * half(j, p, -2))
                    for c in range(TOPK):
                        v.scalar_tensor_tensor(junk[:, c, :], iota_e[:, :], topf[:, c:c + 1], score[:, :],
                                               ALU.is_equal, ALU.mult, accum_out=entry[p][:, c, 1:2])
                    v.tensor_copy(entry[p][:, :, 0], dest_all[:, bass.ds(u, 1)].broadcast_to([P, TOPK]))
                u = t - 1
                if valid(u):
                    dve.wait_ge(o_back, u + 1)
                    wait(dve, oT_ps, u)
                    po = PS[:, O_BANK, :].rearrange("p (h w) -> p h w", w=HP)
                    link(v.reciprocal(rden[:, :], po[:, :, HD]))
                    v.tensor_tensor(o_n[:, :].rearrange("p (h s) -> p h s", s=HD), po[:, :, 0:HD],
                                    spread(rden[:, :], 2, HD),
                                    ALU.mult).then_inc(o_ready, 1)
                u = t + 1
                if valid(u):
                    dve.wait_ge(rstd_qk, u + 1)
                    wait(dve, k_ps, u)
                    v.tensor_tensor(qkn[:, :, 0:HD], PS[:, QK_BANK, :].rearrange("p (h s) -> p h s", s=HD),
                                    spread(rqk[:, :], 2, HD),
                                    ALU.mult).then_inc(qkn_ready, 1)
                u = t + 3
                if valid(u):
                    dve.wait_ge(rstd_a, u + 1)
                    wait(dve, aT_ps, u - 1)
                    normalize(a_n[q][:, :], row(u), 1).then_inc(a_ready, 1)
                u = t + 1
                if valid(u):
                    dve.wait_ge(k_ps, u + 1)
                    if not isinstance(u, int) or u >= 2:
                        dve.wait_ge(st_done, RG * (u - 1))
                    v.tensor_scalar(kT[q][:, :, :].rearrange("p g s -> p (g s)"), PS[:, QK_BANK, :],
                                    cols_sb[:, 2:3], cols_sb[:, 3:4], ALU.mult, ALU.add).then_inc(k_ready, 1)
                clear()
            attention(dve, step)

            k[0] = 0

            def link(ins):
                k[0] += 1
                ins.then_inc(route_step, 1)
                dve.wait_ge(route_step, k[0])
            dve.wait_ge(counts_done, 1)
            counts = PS[:, O_BANK, RANK_AT:RANK_AT + E]
            link(v.tensor_tensor(over[:, :, :], spread(counts, 2, RB),
                                 spread(steps16[:, :], 1, E), ALU.is_gt))
            link(v.tensor_reduce(ntile[:, 0, :], over[:, :, :], axis=AX.X, op=ALU.add))
            for i, s in enumerate((1, 2, 4)):
                v.tensor_copy(ntile[:, i + 1, 0:s], ntile[:, i, 0:s])
                link(v.tensor_tensor(ntile[:, i + 1, s:E], ntile[:, i, s:E], ntile[:, i, 0:E - s], ALU.add))
            ends = ntile[:, 3, :]
            link(v.tensor_scalar(ended[:, 0, :], ends, tile_no[:, :], 0.0, ALU.is_le, ALU.add,
                                 accum_out=erow[:, 0:1]))
            link(v.tensor_tensor(ended[:, 1, :], ended[:, 0, :], ntile[:, 0, :], ALU.mult))
            link(v.tensor_reduce(erow[:, 1:2], ended[:, 1, :], axis=AX.X, op=ALU.add))
            link(v.tensor_tensor(erow[:, 2:3], tile_no[:, :], erow[:, 1:2], ALU.subtract))
            link(v.scalar_tensor_tensor(erow[:, 3:4], erow[:, 0:1], float(RB), erow[:, 2:3], ALU.mult, ALU.add))
            v.tensor_copy(rowi[:, :], erow[:, 3:4]).then_inc(rowi_ready, 1)
            link(v.tensor_tensor(le8[:, :, :], spread(ntile[0:1, 3, :], 1, NTP),
                                 spread(tile_row[:, :], 2, E), ALU.is_le))
            link(v.tensor_reduce(er[:, 0, :], le8[:, :, :], axis=AX.X, op=ALU.add))
            link(v.tensor_scalar(er[:, 1, :], er[:, 0, :], float(E - 1), None, ALU.min))
            v.tensor_copy(er_i[:, :], er[:, 1, :]).then_inc(er_ready, 1)
            dve.wait_ge(tab_tr, 1)
            v.tensor_copy(slot_score[:, :], PS[:, T_BANK, P:P + NTP])
            v.tensor_copy(dest_i[:, :], PS[:, T_BANK, 0:NTP])
            link(v.tensor_copy(dest[:, 0, :], PS[:, T_BANK, 0:NTP]))
            link(v.tensor_scalar(dest[:, 1, :], dest[:, 0, :], float(TOK), float(TOK), ALU.is_ge, ALU.mult))
            link(v.tensor_tensor(dest[:, 0, :], dest[:, 0, :], dest[:, 1, :], ALU.subtract))
            v.tensor_copy(src_i[:, :], dest[:, 0, :]).then_inc(slots_ready, 1)

            def scale(t, p, n):
                dve.wait_ge(xg_loaded[p], 16 * n)
                v.tensor_scalar(xg_sb[p], xg_sb[p], slot_score[:, bass.ds(t, 1)], None, ALU.mult).then_inc(xs_ready, 1)

            def times(t, p):
                dve.wait_ge(silu_ready, t + 1)
                hp = h_sb[p].rearrange("p (c n) -> p c n", c=2)
                v.tensor_tensor(hp, hp, PS[:, 2:4, 0:FH], ALU.mult).then_inc(hh_ready, 1)

            def h_out(t, p):
                dve.wait_ge(hT_tr, t + 1)
                v.tensor_copy(hT_sb[p][:, 4, :], PS[:, 5, 0:P])
                v.tensor_copy(hT_sb[p][0:FT, 5, :], PS[0:FT, 5, P:2 * P]).then_inc(hT_v_ready, 1)

            def y_out(t, p, stored):
                dve.wait_ge(w2_done, t + 1)
                if stored is not None:
                    dve.wait_ge(y_stored[p], 16 * stored)
                v.tensor_copy(y_sb[p][:, :], PS[:, 7, 0:D]).then_inc(y_ready, 1)

            def expert_step(t, p, j):
                scale(t + 1, 1 - p, j + 2)
                times(t, p)
                y_out(t - 1, 1 - p, None if isinstance(t, int) and t <= 2 else j)
                h_out(t, p)
            scale(0, 0, 1)
            scale(1, 1, 1)
            times(0, 0)
            h_out(0, 0)
            experts(dve, 1, 3, expert_step)
            y_out(NT - 1, 0, NT // 2)

        @block.tensor
        def _(pe):
            n = nc.tensor

            def transposes(src, count, width=P, rows=P, bank=T_BANK, at=0):
                for i in range(count):
                    last = n.transpose(PS[0:width, bank, at + i * rows:at + (i + 1) * rows],
                                       src[:, i * width:(i + 1) * width], ident[0:rows, 0:rows])
                return last

            def values(u, p, heads):
                for h in heads:
                    r, g = h % RG, h // RG
                    at = (r * GROUPS + g) * P
                    last = n.matmul(PS[HP * r:HP * r + HP, O_BANK, g * P:(g + 1) * P], v_aug[p][:, h, :],
                                    work[p][:, at:at + P], start=True, stop=True)
                return last

            def step(t, p, j):
                edge = isinstance(t, int)
                if edge and t == 0:
                    pe.wait_ge(prep_done, 2 + DK)
                if valid(t):
                    for r in range(RG):
                        if not edge or t > 0:
                            pe.wait_ge(exp_done, RG * (t - 1) + r + 1)
                        n.matmul(PS[:, r, :], identb[:, :],
                                 spread(mask_qk[:, :], 1, GROUPS),
                                 start=True, stop=True)
                    pe.wait_ge(q_ready, t + 1)
                    pe.wait_ge(k_ready, t + 1)
                    for g in range(GROUPS):
                        for r in range(RG):
                            rows = slice(HP * r, HP * r + HP)
                            last = n.matmul(PS[:, r, g * P:(g + 1) * P], qT[p][rows, g, :], kT[p][rows, g, :],
                                            start=False, stop=True, skip_group_check=True)
                            if g == GROUPS - 1:
                                last.then_inc(s_done, 1)
                u = t + 1
                if valid(u):
                    pe.wait_ge(aT_ready, u + 1)
                    wait(pe, k_ready, u)
                    wait(pe, v_ready, u)
                    wait(pe, var_f, u - 2)
                    for bank, w0, w, done in ((QK_BANK, 0, 2 * D, qk_done), (VY_BANK, 2 * D, D, v_done)):
                        for k in range(DK):
                            last = n.matmul(PS[:, bank, 0:w], aT[:, k, :], wqkv_sb[:, k, w0:w0 + w],
                                            start=(k == 0), stop=(k == DK - 1))
                        last.then_inc(done, 1)
                u = t - 2
                if valid(u):
                    wait(pe, q_ready, t + 1)
                    if edge:
                        wait(pe, gexp_ready, u)
                    pe.wait_ge(x2_ready, u + 1)
                    transposes(x2[p], DK).then_inc(x2T_ps, 1)
                u = t - 1
                if valid(u):
                    pe.wait_ge(exp_done, RG * u + RG)
                    pe.wait_ge(v_ready, u + 1)
                    wait(pe, slot_ready, u - 1)
                    wait(pe, aT_ready, t + 2)
                    wait(pe, oT_ready, u)
                    values(u, 1 - p, range(H)).then_inc(pv_done, 1)
                if valid(t):
                    pe.wait_ge(m3_ready, t + 1)
                    if valid(t - 2):
                        pe.wait_ge(x2T_ready, t - 1)
                    n.transpose(mT_ps, m3[:, :, :].rearrange("p i c -> p (i c)"), identb[:, :]).then_inc(mT_tr, 1)
                u = t - 2
                if valid(u):
                    pe.wait_ge(x2T_ready, u + 1)
                    for k in range(DK):
                        last = n.matmul(PS[:, T_BANK, GATE_AT:GATE_AT + E], x2T[:, k, :], gate_sb[:, k, :],
                                        start=(k == 0), stop=(k == DK - 1))
                    last.then_inc(gate_done, 1)
                if valid(t):
                    pe.wait_ge(max_done, RG * t + RG)
                    for r in range(RG):
                        n.matmul(PS[:, r, :], identb[:, :],
                                 spread(mask_kq[:, :], 1, GROUPS),
                                 start=True, stop=True)
                u = t - 1
                if valid(u):
                    pe.wait_ge(o_raw_ready, u + 1)
                    transposes(o_raw, GROUPS, bank=O_BANK).then_inc(o_back, 1)
                if valid(t):
                    pe.wait_ge(mT_ready, t + 1)
                    for g in range(GROUPS):
                        for r in range(RG):
                            n.matmul(PS[:, r, g * P:(g + 1) * P], sel[:, r * GROUPS + g, :], mT[:, :],
                                     start=False, stop=True, skip_group_check=True)
                        for r in range(RG):
                            rows = slice(HP * r, HP * r + HP)
                            last = n.matmul(PS[:, r, g * P:(g + 1) * P], kT[p][rows, g, :], qT[p][rows, g, :],
                                            start=False, stop=True, skip_group_check=True)
                            if g == GROUPS - 1:
                                last.then_inc(st_done, 1)
                u = t - 1
                if valid(u):
                    pe.wait_ge(o_ready, u + 1)
                    transposes(o_n, DK, bank=O_BANK).then_inc(oT_ps, 1)
                u = t + 1
                if valid(u):
                    pe.wait_ge(qkn_ready, u + 1)
                    flat = qkn[:, :, :].rearrange("p h s -> p (h s)")
                    wait(pe, mT_ready, t + 1)
                    wait(pe, gexp_ready, t - 1)
                    transposes(flat[:, 0:H * HP], GROUPS).then_inc(q_ps, 1)
                    transposes(flat[:, H * HP:2 * H * HP], GROUPS, bank=QK_BANK).then_inc(k_ps, 1)
                u = t - 1
                if valid(u):
                    pe.wait_ge(oT_ready, u + 1)
                    wait(pe, var_f, u)
                    wait(pe, v_ready, t + 2)
                    for k in range(DK):
                        last = n.matmul(PS[:, VY_BANK, D:2 * D], oT[:, k, :], wo_sb[:, k, :],
                                        start=(k == 0), stop=(k == DK - 1))
                    last.then_inc(wo_done, 1)
                u = t - 2
                if valid(u):
                    pe.wait_ge(chosen_ready, u + 1)
                    wait(pe, sum_ready, u)
                    wait(pe, oT_ready, t)
                    wait(pe, slot_ready, u)
                    wait(pe, aT_ready, t + 2)
                    ranks = PS[:, O_BANK, RANK_AT:RANK_AT + E]
                    n.matmul(ranks, upper[:, :], chosen[p][:, :], start=True, stop=False)
                    n.matmul(ranks, onesb[:, :], chosen_sum[p][:, :], start=False, stop=True).then_inc(rank_done, 1)
                u = t + 2
                if valid(u):
                    pe.wait_ge(a_ready, u + 1)
                    wait(pe, oT_ready, t)
                    wait(pe, aT_ready, u)
                    transposes(a_n[p], DK, bank=O_BANK).then_inc(aT_ps, 1)

            pe.wait_ge(pool_const, 2)
            pe.wait_ge(prep_done, 1 + DK)
            attention(pe, step)

            pe.wait_ge(sum_ready, B)
            pe.wait_ge(slot_ready, B)
            n.matmul(PS[:, O_BANK, RANK_AT:RANK_AT + E], onesb[:, :], chosen_sum[0][:, :],
                     start=True, stop=True).then_inc(counts_done, 1)
            pe.wait_ge(trow_loaded, 16)
            for c in range(2):
                last = n.transpose(PS[:, T_BANK, c * P:c * P + NTP], trow[:, :, c], ident[0:NTP, 0:NTP])
            last.then_inc(tab_tr, 1)
            pe.wait_ge(er_ready, 1)
            pe.wait_ge(slots_ready, 1)
            pe.wait_ge(ld_ffn, 16 * 4 * E)

            def x_in_t(t, p):
                pe.wait_ge(xs_ready, t + 1)
                if not isinstance(t, int) or t > 0:
                    pe.wait_ge(xT_ready, t)
                transposes(xg_sb[p], DK).then_inc(xT_tr, 1)

            def up(t, p, e):
                pe.wait_ge(xT_ready, t + 1)
                if not isinstance(t, int) or t > 0:
                    pe.wait_ge(silu_ready, t)
                    pe.wait_ge(hh_ready, t)
                for c in range(4):
                    for k in range(DK):
                        last = n.matmul(PS[:, c, 0:FH], xT_sb[p][:, k, :],
                                        w13_sb[:, bass.ds(e, 1), k, c * FH:(c + 1) * FH],
                                        start=(k == 0), stop=(k == DK - 1))
                last.then_inc(w13_done, 1)

            def h_t(t, p):
                pe.wait_ge(hh_ready, t + 1)
                if not isinstance(t, int) or t > 0:
                    pe.wait_ge(hT_a_ready, t)
                    pe.wait_ge(hT_v_ready, t)
                for i in range(FK):
                    w = min(P, F - i * P)
                    last = n.transpose(PS[0:w, 4 + i // 4, i % 4 * P:(i % 4 + 1) * P],
                                       h_sb[p][:, i * P:i * P + w], ident[:, :])
                last.then_inc(hT_tr, 1)

            def down(t, p, e):
                pe.wait_ge(hT_a_ready, t + 1)
                pe.wait_ge(hT_v_ready, t + 1)
                if not isinstance(t, int) or t > 0:
                    pe.wait_ge(y_ready, t)
                for i in range(FK):
                    w = min(P, F - i * P)
                    last = n.matmul(PS[:, 7, 0:D], hT_sb[p][0:w, i, :], w2_sb[0:w, bass.ds(e, 1), i, :],
                                    start=(i == 0), stop=(i == FK - 1))
                last.then_inc(w2_done, 1)

            def expert_of(t):
                return pe.value_load(er_i[0:1, bass.ds(t, 1)], min_val=0, max_val=E - 1)

            def expert_step(t, p, j):
                up(t, p, expert_of(t))
                x_in_t(t + 1, 1 - p)
                down(t - 1, 1 - p, expert_of(t - 1))
                h_t(t, p)
            x_in_t(0, 0)
            up(0, 0, expert_of(0))
            x_in_t(1, 1)
            h_t(0, 0)
            experts(pe, 1, 3, expert_step)
            down(NT - 1, 0, expert_of(NT - 1))


def kernel(**inputs):
    import concourse.bacc as bacc
    import numpy as np
    from concourse.bass_utils import run_bass_kernel_spmd

    a = {name: np.asarray(v) for name, v in inputs.items()}

    def padded(v):
        return np.tile(np.concatenate([v, np.zeros(HP - HD, v.dtype)]), RG)

    bias_row = np.zeros(D, np.float32)
    bias_row[0:E] = a["L0_ffn_expert_bias"]
    arrays = {
        "ids": np.ascontiguousarray(a["x"].T),
        "types": np.ascontiguousarray(a["mask_BS_i1_0"].T),
        "word": a["L0_tok_word_emb"],
        "rows": np.concatenate([a["L0_tok_pos_emb"], a["L0_tok_type_emb"], a["L0_tok_gamma"][None],
                                a["L0_tok_beta"][None], a["L0_attn_bo"][None], bias_row[None]]),
        "w_qkv": np.concatenate([a["L0_attn_Wq"], a["L0_attn_Wk"], a["L0_attn_Wv"]], axis=1),
        "w_o": a["L0_attn_Wo"],
        "head_cols": np.stack([padded(a[f"L0_attn_{n}"]) for n in ("qln_w", "qln_b", "kln_w", "kln_b")], axis=1),
        "gate_t": np.ascontiguousarray(a["L0_ffn_gate_w"].T),
        "w1": a["L0_ffn_w1"],
        "w3": a["L0_ffn_w3"],
        "w2": a["L0_ffn_w2"],
    }
    arrays = {name: np.ascontiguousarray(v) for name, v in arrays.items()}
    nc = bacc.Bacc("TRN2", target_bir_lowering=False, num_devices=1)
    args = [nc.dram_tensor(f"{name}_dram", v.shape, mybir.dt.from_np(v.dtype), kind="ExternalInput").ap()
            for name, v in arrays.items()]
    out = nc.dram_tensor("out_dram", (TOK + P, D), mybir.dt.float32, kind="ExternalOutput").ap()
    build_tower(nc, *args, out)
    r = run_bass_kernel_spmd(nc, [{f"{name}_dram": v for name, v in arrays.items()}], core_ids=[0])
    return r.results[0]["out_dram"][0:TOK].reshape(B, P, D)
```

```python
from contextlib import ExitStack

import concourse.bass as bass
import concourse.mybir as mybir

P = 128
B = 16
D = 256
DK = D // P
H = 16
HD = D // H
HP = 32
GROUPS = H * HP // P
RG = P // HP
E = 8
F = 704
FH = F // 2
FK = -(-F // P)
FT = F - (FK - 1) * P
TOK = B * P
TOPK = 2
NT = (TOK * TOPK + E * (P - 1)) // P
NTP = NT + 2
RB = TOK // P
TROWS = E * RB + NTP - TOK * TOPK // P
NEG = -1.0e30
WARM_START, WARM_FIRST, WARM_EXPERTS = 32, 14, 12
QK_BANK, VY_BANK, T_BANK, O_BANK = 4, 5, 6, 7
GATE_AT, RANK_AT = 320, 288


def spread(ap, axis, count):
    ap = ap.unsqueeze(axis)
    shape = list(ap.shape)
    shape[axis] = count
    return ap.broadcast_to(shape)


def build_tower(nc, ids, types, word, rows, w_qkv, w_o, head_cols, gate_t, w1, w3, w2, out):
    f32, bf16, i32, u32 = mybir.dt.float32, mybir.dt.bfloat16, mybir.dt.int32, mybir.dt.uint32
    ALU, ACT, AX = mybir.AluOpType, mybir.ActivationFunctionType, mybir.AxisListType

    x2_dram = nc.dram_tensor("x2_rows", (TOK, D), f32).ap()
    table = nc.dram_tensor("slot_table", (TROWS * P, 2), f32).ap()

    ctx = ExitStack()
    with ctx:
        def sb(name, shape, dt=f32):
            return ctx.enter_context(nc.sbuf_tensor(name, shape, dt))

        def sem(name):
            return ctx.enter_context(nc.semaphore(name))

        w13_sb = sb("w13_sb", [P, E, DK, 2 * F])
        w2_sb = sb("w2_sb", [P, E, FK, D])
        h_all = sb("h_all", [P, B, D])
        wo_sb = sb("wo_sb", [P, DK, D])
        rows_sb = sb("rows_sb", [P, 6, D])
        ebias = sb("ebias", [P, E])
        gate_sb = sb("gate_sb", [P, DK, E])
        cols_sb = sb("cols_sb", [P, 4])
        ids_sb = sb("ids_sb", [P, B], i32)
        types_sb = sb("types_sb", [P, B], i32)
        typesf = sb("typesf", [P, B])
        ident = sb("ident", [P, P])
        identb = sb("identb", [P, P], bf16)
        upper = sb("upper", [P, P], bf16)
        onesb = sb("onesb", [P, P], bf16)
        mask = sb("mask", [P, P], bf16)
        neghalf = sb("neghalf", [P, 2 * H])
        iota_e = sb("iota_e", [P, E])
        slot_base = sb("slot_base", [P, E])
        dest_all = sb("dest_all", [P, B])
        idx = [sb(f"idx{p}", [P, 1], i32) for p in range(2)]
        tcol = sb("tcol", [P, 1])
        zeros = sb("zeros", [P, TOPK])
        x_in = [sb(f"x_in{p}", [P, D]) for p in range(2)]
        x_base = sb("x_base", [P, D])
        tmp = sb("tmp", [P, D])
        st6 = sb("st6", [P, 3, 6])
        mv = sb("mv", [P, 3, 2])
        veps = sb("veps", [P, 3])
        rstd = sb("rstd", [P, 3])
        a_n = [sb(f"a_n{p}", [P, D]) for p in range(2)]
        aT = [sb(f"aT{p}", [P, DK, P]) for p in range(2)]
        v_aug = [sb(f"v_aug{p}", [P, H, HP]) for p in range(2)]
        o_raw = sb("o_raw", [P, GROUPS * P])
        ss = sb("ss", [P, 2 * H])
        sse = sb("sse", [P, 2 * H])
        rqk = sb("rqk", [P, 2 * H])
        qkn = sb("qkn", [P, 2 * H, HP])
        nmax = sb("nmax", [P, H])
        work = [sb(f"work{p}", [P, 4 * 512]) for p in range(2)]
        rden = sb("rden", [P, H])
        oT = sb("oT", [P, DK, P])
        x2 = [sb(f"x2_{p}", [P, D]) for p in range(2)]
        x2T = sb("x2T", [P, DK, P])
        gneg = sb("gneg", [P, 1])
        gexp = sb("gexp", [P, E])
        gsum = sb("gsum", [P, 1])
        grs = sb("grs", [P, 1])
        score = sb("score", [P, E])
        biased = sb("biased", [P, E])
        top8 = sb("top8", [P, 8])
        topi = sb("topi", [P, 8], u32)
        topf = sb("topf", [P, TOPK])
        oh0 = sb("oh0", [P, E])
        junk = sb("junk", [P, 2, E])
        chosen = [sb(f"chosen{p}", [P, E], bf16) for p in range(2)]
        chosen_sum = [sb(f"chosen_sum{p}", [P, E], bf16) for p in range(2)]
        ranked = sb("ranked", [P, E])
        slotf = [sb(f"slotf{p}", [P, TOPK]) for p in range(2)]
        sloti = [sb(f"sloti{p}", [P, TOPK], i32) for p in range(2)]
        entry = [sb(f"entry{p}", [P, TOPK, 2]) for p in range(2)]
        steps16 = sb("steps16", [P, RB])
        ntile = sb("ntile", [P, 4, E])
        tile_no = sb("tile_no", [P, 1])
        tile_row = sb("tile_row", [1, NTP])
        ended = sb("ended", [P, 2, E])
        erow = sb("erow", [P, 4])
        rowi = sb("rowi", [P, 1], i32)
        er = sb("er", [1, 2, NTP])
        er_i = sb("er_i", [1, NTP], i32)
        dest = sb("dest", [P, 2, NTP])
        dest_i = sb("dest_i", [P, NTP], i32)
        src_i = sb("src_i", [P, NTP], i32)
        slot_score = sb("slot_score", [P, NTP])
        src_c = [sb(f"src_c{p}", [P, 1], i32) for p in range(2)]
        dst_c = [sb(f"dst_c{p}", [P, 1], i32) for p in range(2)]
        PS = ctx.enter_context(nc.psum_tensor("PS", [P, 8, 512], f32))

        wqkv_sb = w2_sb[:, E - 1, :, :].rearrange("p k d -> p (k d)").rearrange("p (k n) -> p k n", k=DK)
        prep = o_raw[:, 0:2 * DK * H]
        late = w13_sb[:, E - 1, :, :].rearrange("p k n -> p (k n)")
        qT, kT = ([late[:, (2 * i + p) * 512:(2 * i + p + 1) * 512].rearrange("p (g s) -> p g s", s=P)
                   for p in range(2)] for i in range(2))
        sq = late[:, 2048:2560]
        o_n = rows_sb[:, 1, :]
        over = work[1][:, 0:E * RB].rearrange("p (e j) -> p e j", e=E)
        le8 = work[1][0:1, 128:128 + NTP * E].rearrange("p (t e) -> p t e", e=E)
        trow = work[1][0:NTP, 512:512 + 2 * P].rearrange("p (s c) -> p s c", c=2)

        pos_t0, type_diff = rows_sb[:, 0, :], rows_sb[:, 2, :]
        gamma, beta, bo = rows_sb[:, 3, :], rows_sb[:, 4, :], rows_sb[:, 5, :]
        probs, probsT = work[0], work[1]
        init_rows = work[0][:, 0:2 * P].rearrange("p (s c) -> p s c", c=2)
        zero_rows = work[1][:, 0:D]

        late_ranks, counts = PS[:, QK_BANK, 0:E], PS[:, QK_BANK, E:2 * E]

        def part(p, at, n):
            return work[p][:, at:at + n]
        XG, XT, HH, HT = 0, 256, 512, 512 + F
        hT_sb = [part(p, HT, FK * P).rearrange("p (k s) -> p k s", k=FK) for p in range(2)]
        h_sb = [part(p, HH, F) for p in range(2)]
        xg_sb = [part(p, XG, D) for p in range(2)]
        xT_sb = [part(p, XT, D).rearrange("p (k s) -> p k s", k=DK) for p in range(2)]
        y_sb = x_in

        ld_ids, ld_first, ld_small = sem("ld_ids"), sem("ld_first"), sem("ld_small")
        ld_qkv, ld_rest, ld_ffn = sem("ld_qkv"), sem("ld_rest"), sem("ld_ffn")
        pool_const, pool_step = sem("pool_const"), sem("pool_step")
        prep_done, prep_step = sem("prep_done"), sem("prep_step")
        table_init = sem("table_init")
        gathered = [sem(f"gathered{p}") for p in range(2)]
        pool_chain, dve_chain = sem("pool_chain"), sem("dve_chain")
        x_base_ready, x_summed, pool_bo = sem("x_base_ready"), sem("x_summed"), sem("pool_bo")
        var_e, var_a, var_f, var_qk = sem("var_e"), sem("var_a"), sem("var_f"), sem("var_qk")
        rstd_e, rstd_a, rstd_f, rstd_qk = sem("rstd_e"), sem("rstd_a"), sem("rstd_f"), sem("rstd_qk")
        x_used, a_ready = sem("x_used"), sem("a_ready")
        chosen_ready, slot_ready = sem("chosen_ready"), sem("slot_ready")
        aT_ps, aT_ready, qk_done, v_done, v_ready, sq_ready = (
            sem("aT_ps"), sem("aT_ready"), sem("qk_done"), sem("v_done"), sem("v_ready"), sem("sq_ready"))
        qkn_ready, q_ps, k_ps, q_ready, k_ready = (
            sem("qkn_ready"), sem("q_ps"), sem("k_ps"), sem("q_ready"), sem("k_ready"))
        s_done, max_done, exp_done = sem("s_done"), sem("max_done"), sem("exp_done")
        probsT_ps, probsT_ready, pv_done, o_ready = (
            sem("probsT_ps"), sem("probsT_ready"), sem("pv_done"), sem("o_ready"))
        o_raw_ready, o_back = sem("o_raw_ready"), sem("o_back")
        oT_ps, oT_ready, wo_done = sem("oT_ps"), sem("oT_ready"), sem("wo_done")
        x2_ready, x2T_ps, x2T_ready = sem("x2_ready"), sem("x2T_ps"), sem("x2T_ready")
        x2_stored = [sem(f"x2_stored{p}") for p in range(2)]
        gate_done, gneg_ready, gexp_ready = sem("gate_done"), sem("gneg_ready"), sem("gexp_ready")
        rank_done, sum_ready = sem("rank_done"), sem("sum_ready")
        scattered = [sem(f"scattered{p}") for p in range(2)]
        counts_done, rowi_ready, route_step, er_ready = (
            sem("counts_done"), sem("rowi_ready"), sem("route_step"), sem("er_ready"))
        trow_loaded, tab_tr, slots_ready, slots_read = (
            sem("trow_loaded"), sem("tab_tr"), sem("slots_ready"), sem("slots_read"))
        xg_loaded = [sem(f"xg_loaded{p}") for p in range(2)]
        xs_ready, xT_tr, xT_ready = sem("xs_ready"), sem("xT_tr"), sem("xT_ready")
        w13_done, silu_ready, hh_ready = sem("w13_done"), sem("silu_ready"), sem("hh_ready")
        hT_tr, hT_a_ready, hT_v_ready = sem("hT_tr"), sem("hT_a_ready"), sem("hT_v_ready")
        w2_done, y_ready = sem("w2_done"), sem("y_ready")
        y_stored = [sem(f"y_stored{p}") for p in range(2)]
        h_stored = sem("h_stored")

        block = ctx.enter_context(nc.Block())

        def wait(eng, s, n):
            if isinstance(n, int):
                n = min(n, B)
                if n <= 0:
                    return
            eng.wait_ge(s, n)

        def chain(eng, s):
            k = [0]

            def link(ins):
                k[0] += 1
                ins.then_inc(s, 1)
                eng.wait_ge(s, k[0])

            def clear():
                eng.sem_clear(s)
            return link, clear

        AHEAD, BEHIND = 4, 3
        LOOP = 4

        def valid(t):
            return not isinstance(t, int) or 0 <= t < B

        def half(j, p, ahead):
            return j + (p + ahead) // 2

        def attention(eng, step):
            for t in range(-AHEAD, LOOP):
                step(t, t % 2, t // 2)
            with eng.Fori(LOOP // 2, (B - AHEAD) // 2) as j:
                for p in range(2):
                    step(2 * j + p, p, j)
            for t in range(B - AHEAD, B + BEHIND):
                step(t, t % 2, t // 2)

        def experts(eng, first, loop_first, step):
            for t in range(first, loop_first):
                step(t, t % 2, (t - 1) // 2)
            with eng.Fori((loop_first - 1) // 2, (NT - 1) // 2) as j:
                for i in range(2):
                    step(2 * j + 1 + i, 1 - i, j)

        @block.sync
        def _(sp):
            sp.dma_start(ids_sb[:, :], ids).then_inc(ld_ids, 16)
            sp.dma_start(types_sb[:, :], types).then_inc(ld_first, 16)
            sp.dma_start(rows_sb[:, 0, :], rows[0:P, :]).then_inc(ld_first, 16)
            sp.dma_start(rows_sb[:, 1:3, :],
                         spread(rows[P:P + 2, :], 0, P)).then_inc(ld_first, 16)
            sp.dma_start(rows_sb[:, 3:6, :],
                         spread(rows[P + 2:P + 5, :], 0, P)).then_inc(ld_small, 16)
            sp.dma_start(ebias[:, :], spread(rows[P + 5, 0:E], 0, P)).then_inc(ld_small, 16)
            sp.dma_start(cols_sb[:, :], head_cols).then_inc(ld_small, 16)
            sp.wait_ge(pool_const, 1)
            sp.dma_start(table[0:P * P, :].rearrange("(r s) c -> r (s c)", s=P),
                         init_rows.rearrange("p s c -> p (s c)")).then_inc(table_init, 16)
            sp.dma_start(table[P * P:TROWS * P, :].rearrange("(r s) c -> r (s c)", s=P),
                         init_rows[0:TROWS - P].rearrange("p s c -> p (s c)")).then_inc(table_init, 16)
            sp.dma_start(out[TOK:TOK + P, :], zero_rows).then_inc(table_init, 16)

            expert_at = dict(zip((*range(LOOP), *range(B - AHEAD, B + BEHIND)), range(E - 1)))

            def load_expert(e):
                sp.dma_start(w13_sb[:, e, :, 0:F], w1[e].rearrange("(k p) n -> p k n", p=P)).then_inc(ld_ffn, 16)
                sp.dma_start(w13_sb[:, e, :, F:2 * F], w3[e].rearrange("(k p) n -> p k n", p=P)).then_inc(ld_ffn, 16)
                sp.dma_start(w2_sb[:, e, 0:FK - 1, :],
                             w2[e, 0:F - FT].rearrange("(k p) n -> p k n", p=P)).then_inc(ld_ffn, 16)
                sp.dma_start(w2_sb[0:FT, e, FK - 1, :], w2[e, F - FT:F]).then_inc(ld_ffn, 16)

            def step(t, p, j):
                u = t - 2
                if valid(u):
                    sp.wait_ge(x2_ready, u + 1)
                    sp.dma_start(x2_dram[bass.ds(u * P, P), :], x2[p][:, :]).then_inc(x2_stored[p], 16)
                    sp.dma_start(out[bass.ds(u * P, P), :],
                                 h_all[:, bass.ds(u, 1), :].rearrange("p o d -> p (o d)")).then_inc(h_stored, 16)
                if isinstance(t, int) and t in expert_at:
                    sp.wait_ge(x_summed, min(t + AHEAD, B))
                    load_expert(expert_at[t])
            attention(sp, step)

            sp.wait_ge(v_done, B)
            sp.wait_ge(var_qk, B)
            sp.wait_ge(s_done, RG * B)
            load_expert(E - 1)

        @block.gpsimd
        def _(pool):
            g = nc.gpsimd
            k = [0]

            def link(ins):
                k[0] += 1
                ins.then_inc(pool_step, 1)
                pool.wait_ge(pool_step, k[0])
            g.memset(zero_rows, 0.0)
            link(g.memset(init_rows, 0.0))
            g.memset(neghalf[:, :], -0.5)
            g.iota(init_rows[:, :, 0], pattern=[[1, P]], base=TOK, channel_multiplier=0,
                   allow_small_or_imprecise_dtypes=True).then_inc(pool_const, 1)

            def constants_1():
                link(g.memset(ident[:, :], 0.0))
                link(g.affine_select(out=ident[:, :], in_=ident[:, :], compare_op=ALU.not_equal, fill=1.0,
                                     base=0, pattern=[[-1, P]], channel_multiplier=1))
                g.tensor_copy(identb[:, :], ident[:, :])
                for p in range(2):
                    g.memset(v_aug[p][:, :, HD:HP], 1.0)
                g.memset(qkn[:, :, :], 0.0).then_inc(pool_const, 1)

            def constants_2():
                g.memset(mask[:, :], 0.0)
                link(g.memset(onesb[:, :], 1.0))
                g.affine_select(out=mask[:, :], in_=mask[:, :], compare_op=ALU.is_ge, fill=NEG,
                                base=0, pattern=[[-1, P]], channel_multiplier=1)
                g.affine_select(out=upper[:, :], in_=onesb[:, :], compare_op=ALU.is_gt, fill=0.0,
                                base=0, pattern=[[1, P]], channel_multiplier=-1)
                exact = dict(allow_small_or_imprecise_dtypes=True)
                g.iota(iota_e[:, :], pattern=[[1, E]], base=0, channel_multiplier=0, **exact)
                g.iota(slot_base[:, :], pattern=[[TOK, E]], base=0, channel_multiplier=0, **exact)
                g.iota(dest_all[:, :], pattern=[[P, B]], base=0, channel_multiplier=1, **exact)
                g.iota(steps16[:, :], pattern=[[P, RB]], base=0, channel_multiplier=0, **exact)
                g.iota(tile_no[:, :], pattern=[[0, 1]], base=0, channel_multiplier=1, **exact)
                g.iota(tile_row[:, :], pattern=[[1, NTP]], base=0, channel_multiplier=0, **exact)
                g.memset(chosen_sum[0][:, :], 0.0)
                g.memset(zeros[:, :], 0.0).then_inc(pool_const, 1)
            pool.wait_ge(ld_ids, 16)

            def gather(u, p, link):
                wait(pool, x_used, u - 1)
                link(g.tensor_copy(idx[p][:, :], ids_sb[:, bass.ds(u, 1)]))
                g.indirect_dma_start(x_in[p][:, :], None, word,
                                     bass.IndirectOffsetOnAxis(idx[p][:, :], 0)).then_inc(gathered[p], 16)

            def qk_power(u):
                pool.wait_ge(var_qk, u + 1)
                g.tensor_tensor(rqk[:, :], sse[:, :], neghalf[:, :], ALU.pow).then_inc(rstd_qk, 1)

            def step(t, p, j):
                link, clear = chain(pool, pool_chain)
                u = t - 2
                if valid(u):
                    pool.wait_ge(var_f, u + 1)
                    g.tensor_tensor(rstd[:, 2:3], veps[:, 2:3], neghalf[:, 0:1], ALU.pow).then_inc(rstd_f, 1)
                u = t + 3
                if valid(u):
                    pool.wait_ge(var_e, u + 1)
                    g.tensor_tensor(rstd[:, 0:1], veps[:, 0:1], neghalf[:, 0:1], ALU.pow).then_inc(rstd_e, 1)
                u = t + 4
                if isinstance(t, int) and t == -AHEAD:
                    gather(u, p, link)
                    constants_1()
                    pool.wait_ge(prep_done, 1)
                if valid(u):
                    wait(pool, x_summed, u)
                    link(g.tensor_copy(tcol[:, :], typesf[:, bass.ds(u, 1)]))
                    link(g.tensor_scalar(x_base[:, :], type_diff, tcol[:, :], None, ALU.mult))
                    g.tensor_tensor(x_base[:, :], x_base[:, :], pos_t0, ALU.add).then_inc(x_base_ready, 1)
                u = t + 2
                if valid(u):
                    pool.wait_ge(a_ready, u + 1)
                    hu = h_all[:, bass.ds(u, 1), :].rearrange("p o d -> p (o d)")
                    g.tensor_tensor(hu, hu, bo, ALU.add).then_inc(pool_bo, 1)
                u = t + 3
                if valid(u):
                    pool.wait_ge(var_a, u + 1)
                    g.tensor_tensor(rstd[:, 1:2], veps[:, 1:2], neghalf[:, 0:1], ALU.pow).then_inc(rstd_a, 1)
                if valid(t + 2):
                    qk_power(t + 2)
                u = t + 4
                if valid(u) and not (isinstance(t, int) and t == -AHEAD):
                    gather(u, p, link)
                u = t - 3
                if valid(u):
                    q = 1 - p
                    if isinstance(u, int) and u == 0:
                        pool.wait_ge(table_init, 48)
                    pool.wait_ge(slot_ready, u + 1)
                    link(g.tensor_tensor(slotf[q][:, :], slotf[q][:, :], zeros[:, :], ALU.add))
                    link(g.tensor_copy(sloti[q][:, :], slotf[q][:, :]))
                    for c in range(TOPK):
                        g.indirect_dma_start(table, bass.IndirectOffsetOnAxis(sloti[q][:, c:c + 1], 0),
                                             entry[q][:, c, :], None).then_inc(scattered[q], 16)
                clear()
                if isinstance(t, int) and t == 1 - AHEAD:
                    constants_2()

            attention(pool, step)

            for p in range(2):
                pool.wait_ge(scattered[p], 16 * TOPK * B // 2)
            pool.wait_ge(rowi_ready, 1)
            g.indirect_dma_start(trow[:, :, :].rearrange("t s c -> t (s c)"), None,
                                 table.rearrange("(r s) c -> r (s c)", s=P),
                                 bass.IndirectOffsetOnAxis(rowi[0:NTP, :], 0)).then_inc(trow_loaded, 16)
            pool.wait_ge(slots_ready, 1)
            for p in range(2):
                pool.wait_ge(x2_stored[p], 16 * B // 2)
            pool.wait_ge(h_stored, 16 * B)

            def gather_tile(t, p, link):
                link(g.tensor_copy(src_c[p][:, :], src_i[:, bass.ds(t, 1)]))
                g.indirect_dma_start(xg_sb[p], None, x2_dram,
                                     bass.IndirectOffsetOnAxis(src_c[p][:, :], 0)).then_inc(xg_loaded[p], 16)

            def scatter(t, p, link):
                pool.wait_ge(y_ready, t + 1)
                link(g.tensor_copy(dst_c[p][:, :], dest_i[:, bass.ds(t, 1)]))
                g.indirect_dma_start(out, bass.IndirectOffsetOnAxis(dst_c[p][:, :], 0), y_sb[p][:, :],
                                     None, compute_op=ALU.add).then_inc(y_stored[p], 16)

            def step(t, p, j):
                link, clear = chain(pool, pool_chain)
                pool.wait_ge(xT_tr, t + 1)
                pool.wait_ge(xg_loaded[p], 16 * (j + 2 - p))
                gather_tile(t + 2, p, link)
                if not isinstance(t, int) or t > 2:
                    pool.wait_ge(y_stored[1 - p], 16 * j)
                if not isinstance(t, int) or t > 1:
                    pool.wait_ge(y_stored[p], 16 * (j + 1 - p))
                scatter(t - 1, 1 - p, link)
                clear()
            link, clear = chain(pool, pool_chain)
            gather_tile(0, 0, link)
            gather_tile(1, 1, link)
            pool.wait_ge(xT_tr, 1)
            pool.wait_ge(xg_loaded[0], 16)
            gather_tile(2, 0, link)
            clear()
            pool.wait_ge(slots_read, 1)
            experts(pool, 1, 3, step)
            for p in range(2):
                pool.wait_ge(y_stored[p], 16 * (NT // 2))
            scatter(NT - 1, 0, chain(pool, pool_chain)[0])
            pool.wait_ge(y_stored[0], 16 * (NT - NT // 2))

        @block.scalar
        def _(act):
            a = nc.scalar
            act.wait_ge(ld_first, 48)
            act.dma_start(wqkv_sb[:, :, :], w_qkv.rearrange("(k p) n -> p k n", p=P)).then_inc(ld_qkv, 16)
            act.dma_start(wo_sb[:, :, :], w_o.rearrange("(k p) n -> p k n", p=P)).then_inc(ld_rest, 16)
            act.dma_start(gate_sb[:, :, :], gate_t.rearrange("(k p) n -> p k n", p=P)).then_inc(ld_rest, 16)

            def exponentials(t, banks):
                for r in banks:
                    act.wait_ge(max_done, RG * t + r + 1)
                    for g in range(GROUPS):
                        c = r * GROUPS + g
                        last = a.activation(probs[:, c * P:(c + 1) * P], PS[:, r, g * P:(g + 1) * P], ACT.Exp,
                                            bias=nmax[:, c:c + 1])
                    last.then_inc(exp_done, 1)

            def transposed(t, banks):
                for r in banks:
                    act.wait_ge(probsT_ps, RG * t + r + 1)
                    a.activation(probsT[:, r * 512:(r + 1) * 512], PS[:, r, :], ACT.Copy).then_inc(probsT_ready, 1)

            def step(t, p, j):
                def outputs_out(u):
                    act.wait_ge(pv_done, u + 1)
                    wait(act, o_back, u)
                    a.activation(o_raw[:, :], PS[:, O_BANK, :], ACT.Copy).then_inc(o_raw_ready, 1)

                def x2_out(u):
                    act.wait_ge(x2T_ps, u + 1)
                    wait(act, gate_done, u)
                    a.activation(x2T[:, :, :].rearrange("p k s -> p (k s)"), PS[:, T_BANK, 0:D],
                                 ACT.Copy).then_inc(x2T_ready, 1)

                def gate_exponentials(u):
                    act.wait_ge(gneg_ready, u + 1)
                    a.activation(gexp[:, :], PS[:, T_BANK, GATE_AT:GATE_AT + E], ACT.Exp, bias=gneg[:, :],
                                 accum_out=gsum[:, :]).then_inc(gexp_ready, 1)

                def normalized_out(u):
                    act.wait_ge(oT_ps, u + 1)
                    wait(act, wo_done, u)
                    a.activation(oT[:, :, :].rearrange("p k s -> p (k s)"), PS[:, O_BANK, 0:D],
                                 ACT.Copy).then_inc(oT_ready, 1)

                if isinstance(t, int) and t >= B:
                    if t == B:
                        outputs_out(B - 1)
                        x2_out(B - 2)
                        normalized_out(B - 1)
                        gate_exponentials(B - 2)
                    elif t == B + 1:
                        x2_out(B - 1)
                        gate_exponentials(B - 1)
                    return
                if valid(t):
                    exponentials(t, (0, 1, 2))
                u = t + 1
                if valid(u):
                    for ps_ready, ready, dst, bank, c in ((q_ps, q_ready, qT, T_BANK, 0),
                                                          (k_ps, k_ready, kT, QK_BANK, 2)):
                        act.wait_ge(ps_ready, u + 1)
                        if not isinstance(u, int) or u >= 2:
                            act.wait_ge(s_done, RG * (u - 1))
                        a.activation(dst[1 - p][:, :, :].rearrange("p g s -> p (g s)"), PS[:, bank, :], ACT.Identity,
                                     scale=cols_sb[:, c:c + 1], bias=cols_sb[:, c + 1:c + 2]).then_inc(ready, 1)
                if valid(t):
                    exponentials(t, (3,))
                if valid(t - 1):
                    outputs_out(t - 1)
                u = t + 2
                if valid(u):
                    act.wait_ge(qk_done, u + 1)
                    wait(act, var_qk, u)
                    a.activation(sq[:, :], PS[:, QK_BANK, :], ACT.Square).then_inc(sq_ready, 1)
                if valid(t - 2):
                    x2_out(t - 2)
                if valid(t):
                    wait(act, pv_done, t)
                    transposed(t, (0, 1))
                u = t + 1
                if valid(u):
                    act.wait_ge(v_done, u + 1)
                    wait(act, pv_done, u - 1)
                    a.activation(v_aug[1 - p][:, :, 0:HD], PS[:, VY_BANK, 0:D].rearrange("p (h s) -> p h s", s=HD),
                                 ACT.Copy).then_inc(v_ready, 1)
                if valid(t - 2):
                    gate_exponentials(t - 2)
                if valid(t - 1):
                    normalized_out(t - 1)
                if valid(t):
                    transposed(t, (2, 3))
                u = t + 3
                if valid(u):
                    act.wait_ge(aT_ps, u + 1)
                    wait(act, v_done, u - 1)
                    a.activation(aT[1 - p][:, :, :].rearrange("p k s -> p (k s)"), PS[:, O_BANK, 0:D],
                                 ACT.Copy).then_inc(aT_ready, 1)

            act.wait_ge(pool_const, 1)
            a.activation(gneg[:, :], neghalf[:, 0:1], ACT.Exp)
            act.wait_ge(pool_const, 2)
            act.wait_ge(ld_small, 48)
            act.wait_ge(table_init, 48)
            act.wait_ge(prep_done, 2)
            attention(act, step)

            def x_out(t, p):
                act.wait_ge(xT_tr, t + 1)
                a.activation(xT_sb[p].rearrange("p k s -> p (k s)"), PS[:, T_BANK, 0:D], ACT.Copy).then_inc(xT_ready, 1)

            def silu(t, p):
                act.wait_ge(w13_done, t + 1)
                a.activation(h_sb[p].rearrange("p (c n) -> p c n", c=2), PS[:, 0:2, 0:FH],
                             ACT.Silu).then_inc(silu_ready, 1)

            def h_out(t, p):
                act.wait_ge(hT_tr, t + 1)
                a.activation(hT_sb[p][:, 0:4, :].rearrange("p k s -> p (k s)"), PS[:, 4, :],
                             ACT.Copy).then_inc(hT_a_ready, 1)

            def expert_step(t, p, j):
                silu(t, p)
                x_out(t + 1, 1 - p)
                h_out(t, p)
            x_out(0, 0)
            expert_step(0, 0, 0)
            experts(act, 1, 1, expert_step)

        @block.vector
        def _(dve):
            v = nc.vector
            k = [0]

            def plink(ins):
                k[0] += 1
                ins.then_inc(prep_step, 1)
                dve.wait_ge(prep_step, k[0])
            dve.wait_ge(ld_first, 48)
            v.tensor_copy(typesf[:, :], types_sb[:, :])
            v.tensor_tensor(pos_t0, pos_t0, rows_sb[:, 1, :], ALU.add)
            v.tensor_tensor(type_diff, type_diff, rows_sb[:, 1, :], ALU.subtract).then_inc(prep_done, 1)
            def scale_queries():
                dve.wait_ge(ld_small, 48)
                v.tensor_scalar(cols_sb[:, 0:2], cols_sb[:, 0:2], HD ** -0.5, None,
                                ALU.mult).then_inc(prep_done, 1)

            def center_weights():
                dve.wait_ge(ld_qkv, 16)
                for kk in range(DK):
                    wqk = wqkv_sb[:, kk, 0:2 * D].rearrange("p (h s) -> p h s", s=HD)
                    mean = prep[:, kk * 2 * H:(kk + 1) * 2 * H]
                    plink(v.tensor_reduce(mean, wqk, axis=AX.X, op=ALU.add))
                    plink(v.tensor_scalar(mean, mean, -1.0 / HD, None, ALU.mult))
                    v.tensor_tensor(wqk, wqk, spread(mean, 2, HD),
                                    ALU.add).then_inc(prep_done, 1)

            def stats(link, src, c, eps, var):
                link(v.bn_stats(st6[:, c, :], src))
                link(v.bn_aggr(mv[:, c, :], st6[:, c, :]))
                v.tensor_scalar(veps[:, c:c + 1], mv[:, c, 1:2], eps, None, ALU.add).then_inc(var, 1)

            def normalize(dst, src, c):
                return v.tensor_scalar(dst, src, mv[:, c, 0:1], rstd[:, c:c + 1], ALU.subtract, ALU.mult)

            def qk_variance(u, link):
                dve.wait_ge(sq_ready, u + 1)
                link(v.tensor_reduce(ss[:, :], sq[:, :].rearrange("p (h s) -> p h s", s=HD), axis=AX.X,
                                     op=ALU.add))
                v.tensor_scalar(sse[:, :], ss[:, :], 1.0 / HD, 1e-5, ALU.mult, ALU.add).then_inc(var_qk, 1)

            def row(u):
                return h_all[:, bass.ds(u, 1), :].rearrange("p o d -> p (o d)")

            def step(t, p, j):
                link, clear = chain(dve, dve_chain)
                q = 1 - p
                first = isinstance(t, int) and t == 1 - AHEAD
                if isinstance(t, int) and t == -2:
                    dve.wait_ge(pool_const, 3)

                def maxima(banks):
                    for r in banks:
                        dve.wait_ge(s_done, RG * t + r + 1)
                        v.tensor_reduce(nmax[:, RG * r:RG * r + RG], PS[:, r, :].rearrange("p (g s) -> p g s", s=P),
                                        axis=AX.X, op=ALU.max, negate=True).then_inc(max_done, 1)
                def add_attention(u):
                    dve.wait_ge(wo_done, u + 1)
                    dve.wait_ge(pool_bo, u + 1)
                    link(v.tensor_tensor(row(u), row(u), PS[:, VY_BANK, D:2 * D], ALU.add))
                    stats(link, row(u), 2, 1e-5, var_f)

                def ffn_input(u, p, j):
                    dve.wait_ge(rstd_f, u + 1)
                    wait(dve, x2T_ps, u - 1)
                    if not isinstance(u, int) or u >= 2:
                        dve.wait_ge(x2_stored[p], 16 * half(j, p, -2))
                    normalize(x2[p][:, :], row(u), 2).then_inc(x2_ready, 1)

                def divide(u):
                    dve.wait_ge(o_back, u + 1)
                    wait(dve, oT_ps, u)
                    po = PS[:, O_BANK, :].rearrange("p (h w) -> p h w", w=HP)
                    link(v.reciprocal(rden[:, :], po[:, :, HD]))
                    v.tensor_tensor(o_n[:, :].rearrange("p (h s) -> p h s", s=HD), po[:, :, 0:HD],
                                    spread(rden[:, :], 2, HD),
                                    ALU.mult).then_inc(o_ready, 1)

                def gate_maximum(u):
                    dve.wait_ge(gate_done, u + 1)
                    v.tensor_reduce(gneg[:, :], PS[:, T_BANK, GATE_AT:GATE_AT + E], axis=AX.X, op=ALU.max,
                                    negate=True).then_inc(gneg_ready, 1)

                def choose(u, p, j):
                    dve.wait_ge(gexp_ready, u + 1)
                    link(v.reciprocal(grs[:, :], gsum[:, :]))
                    link(v.tensor_scalar(score[:, :], gexp[:, :], grs[:, :], None, ALU.mult))
                    link(v.tensor_tensor(biased[:, :], score[:, :], ebias[:, :], ALU.add))
                    link(v.max(top8[:, :], biased[:, :]))
                    link(v.max_index(topi[:, :], top8[:, :], biased[:, :]))
                    link(v.tensor_copy(topf[:, :], topi[:, 0:TOPK]))
                    wait(dve, rank_done, u - 1)
                    link(v.tensor_scalar(oh0[:, :], iota_e[:, :], topf[:, 0:1], None, ALU.is_equal))
                    v.scalar_tensor_tensor(chosen[p][:, :], iota_e[:, :], topf[:, 1:2], oh0[:, :],
                                           ALU.is_equal, ALU.add).then_inc(chosen_ready, 1)
                    if not isinstance(u, int) or u >= 2:
                        dve.wait_ge(scattered[p], 16 * TOPK * half(j, p, -2))
                    for c in range(TOPK):
                        v.scalar_tensor_tensor(junk[:, c, :], iota_e[:, :], topf[:, c:c + 1], score[:, :],
                                               ALU.is_equal, ALU.mult, accum_out=entry[p][:, c, 1:2])
                    v.tensor_copy(entry[p][:, :, 0], dest_all[:, bass.ds(u, 1)].broadcast_to([P, TOPK]))

                def slots(u):
                    dve.wait_ge(rank_done, u + 1)
                    late = isinstance(t, int) and t >= B
                    if not late:
                        wait(dve, gexp_ready, t - 1)
                    ranks = late_ranks if late else PS[:, T_BANK, RANK_AT:RANK_AT + E]
                    v.tensor_tensor(chosen_sum[p][:, :], chosen_sum[q][:, :], chosen[q][:, :],
                                    ALU.add).then_inc(sum_ready, 1)
                    link(v.tensor_tensor(ranked[:, :], ranks, slot_base[:, :], ALU.add))
                    for c in range(TOPK):
                        last = v.scalar_tensor_tensor(junk[:, c, :], iota_e[:, :], topf[:, c:c + 1], ranked[:, :],
                                                      ALU.is_equal, ALU.mult, accum_out=slotf[q][:, c:c + 1])
                    last.then_inc(slot_ready, 1)

                if isinstance(t, int) and t >= B:
                    if t == B:
                        add_attention(B - 2)
                        slots(B - 3)
                        ffn_input(B - 2, p, j)
                        divide(B - 1)
                        gate_maximum(B - 2)
                        add_attention(B - 1)
                        ffn_input(B - 1, q, j + p)
                        choose(B - 2, p, j)
                    elif t == B + 1:
                        gate_maximum(B - 1)
                        slots(B - 2)
                        choose(B - 1, p, j)
                    else:
                        slots(B - 1)
                    clear()
                    return
                if valid(t):
                    maxima((0, 1))
                u = t + 1
                if valid(u):
                    dve.wait_ge(rstd_qk, u + 1)
                    wait(dve, k_ps, u)
                    v.tensor_tensor(qkn[:, :, 0:HD], PS[:, QK_BANK, :].rearrange("p (h s) -> p h s", s=HD),
                                    spread(rqk[:, :], 2, HD),
                                    ALU.mult).then_inc(qkn_ready, 1)
                if valid(t):
                    maxima((2, 3))
                if valid(t - 2):
                    add_attention(t - 2)
                u = t + 3
                if valid(u):
                    x = x_in[q][:, :]
                    dve.wait_ge(x_base_ready, u + 1)
                    dve.wait_ge(gathered[q], 16 * (half(j, p, 3) + 1))
                    v.tensor_tensor(x, x, x_base[:, :], ALU.add).then_inc(x_summed, 1)
                    dve.wait_ge(x_summed, u + 1)
                    stats(link, x, 0, 1e-12, var_e)
                    if first:
                        scale_queries()
                if valid(t - 2):
                    ffn_input(t - 2, p, j)
                if valid(u):
                    dve.wait_ge(rstd_e, u + 1)
                    normalize(tmp[:, :], x_in[q][:, :], 0).then_inc(x_used, 1)
                    dve.wait_ge(x_used, u + 1)
                    link(v.tensor_tensor(tmp[:, :], tmp[:, :], gamma, ALU.mult))
                    link(v.tensor_tensor(row(u), tmp[:, :], beta, ALU.add))
                    stats(link, row(u), 1, 1e-5, var_a)
                    if first:
                        center_weights()
                if valid(t + 2):
                    qk_variance(t + 2, link)
                if valid(t - 1):
                    divide(t - 1)
                if valid(t - 2):
                    gate_maximum(t - 2)
                if valid(u):
                    dve.wait_ge(rstd_a, u + 1)
                    wait(dve, aT_ps, u - 1)
                    normalize(a_n[q][:, :], row(u), 1).then_inc(a_ready, 1)
                if valid(t - 3):
                    slots(t - 3)
                if valid(t - 2):
                    choose(t - 2, p, j)
                clear()
            attention(dve, step)

            k[0] = 0

            def link(ins):
                k[0] += 1
                ins.then_inc(route_step, 1)
                dve.wait_ge(route_step, k[0])
            dve.wait_ge(counts_done, 1)
            link(v.tensor_tensor(over[:, :, :], spread(counts, 2, RB),
                                 spread(steps16[:, :], 1, E), ALU.is_gt))
            link(v.tensor_reduce(ntile[:, 0, :], over[:, :, :], axis=AX.X, op=ALU.add))
            for i, s in enumerate((1, 2, 4)):
                v.tensor_copy(ntile[:, i + 1, 0:s], ntile[:, i, 0:s])
                link(v.tensor_tensor(ntile[:, i + 1, s:E], ntile[:, i, s:E], ntile[:, i, 0:E - s], ALU.add))
            ends = ntile[:, 3, :]
            link(v.tensor_scalar(ended[:, 0, :], ends, tile_no[:, :], 0.0, ALU.is_le, ALU.add,
                                 accum_out=erow[:, 0:1]))
            link(v.tensor_tensor(ended[:, 1, :], ended[:, 0, :], ntile[:, 0, :], ALU.mult))
            link(v.tensor_reduce(erow[:, 1:2], ended[:, 1, :], axis=AX.X, op=ALU.add))
            link(v.tensor_tensor(erow[:, 2:3], tile_no[:, :], erow[:, 1:2], ALU.subtract))
            link(v.scalar_tensor_tensor(erow[:, 3:4], erow[:, 0:1], float(RB), erow[:, 2:3], ALU.mult, ALU.add))
            v.tensor_copy(rowi[:, :], erow[:, 3:4]).then_inc(rowi_ready, 1)
            link(v.tensor_tensor(le8[:, :, :], spread(ntile[0:1, 3, :], 1, NTP),
                                 spread(tile_row[:, :], 2, E), ALU.is_le))
            link(v.tensor_reduce(er[:, 0, :], le8[:, :, :], axis=AX.X, op=ALU.add))
            link(v.tensor_scalar(er[:, 1, :], er[:, 0, :], float(E - 1), None, ALU.min))
            v.tensor_copy(er_i[:, :], er[:, 1, :]).then_inc(er_ready, 1)
            dve.wait_ge(tab_tr, 1)
            rows_to = PS[:, T_BANK, 0:NTP]
            link(v.tensor_scalar(dest[:, 1, :], rows_to, float(TOK), float(TOK), ALU.is_ge, ALU.mult))
            link(v.tensor_tensor(dest[:, 0, :], rows_to, dest[:, 1, :], ALU.subtract))
            v.tensor_copy(src_i[:, :], dest[:, 0, :]).then_inc(slots_ready, 1)
            v.tensor_copy(dest_i[:, :], rows_to)
            v.tensor_copy(slot_score[:, :], PS[:, T_BANK, P:P + NTP]).then_inc(slots_read, 1)
            dve.wait_ge(slots_read, 1)

            def scale(t, p, n):
                dve.wait_ge(xg_loaded[p], 16 * n)
                v.tensor_scalar(xg_sb[p], xg_sb[p], slot_score[:, bass.ds(t, 1)], None, ALU.mult).then_inc(xs_ready, 1)

            def times(t, p):
                dve.wait_ge(silu_ready, t + 1)
                hp = h_sb[p].rearrange("p (c n) -> p c n", c=2)
                v.tensor_tensor(hp, hp, PS[:, 2:4, 0:FH], ALU.mult).then_inc(hh_ready, 1)

            def h_out(t, p):
                dve.wait_ge(hT_tr, t + 1)
                v.tensor_copy(hT_sb[p][:, 4, :], PS[:, 5, 0:P])
                v.tensor_copy(hT_sb[p][0:FT, 5, :], PS[0:FT, 5, P:2 * P]).then_inc(hT_v_ready, 1)

            def y_out(t, p, stored):
                dve.wait_ge(w2_done, t + 1)
                if stored is not None:
                    dve.wait_ge(y_stored[p], 16 * stored)
                v.tensor_copy(y_sb[p][:, :], PS[:, 7, 0:D]).then_inc(y_ready, 1)

            def expert_step(t, p, j):
                scale(t + 1, 1 - p, j + 2)
                times(t, p)
                y_out(t - 1, 1 - p, None if isinstance(t, int) and t <= 2 else j)
                h_out(t, p)
            scale(0, 0, 1)
            scale(1, 1, 1)
            times(0, 0)
            h_out(0, 0)
            experts(dve, 1, 3, expert_step)
            y_out(NT - 1, 0, NT // 2)

        @block.tensor
        def _(pe):
            n = nc.tensor

            def transposes(src, count, width=P, rows=P, bank=T_BANK, at=0):
                for i in range(count):
                    last = n.transpose(PS[0:width, bank, at + i * rows:at + (i + 1) * rows],
                                       src[:, i * width:(i + 1) * width], ident[0:rows, 0:rows])
                return last

            def keep_warm(count):
                for _ in range(count):
                    n.matmul(PS[:, 0, :], identb[:, :], spread(identb[:, :], 1, GROUPS), start=True, stop=True)

            def values(u, p, heads):
                for h in heads:
                    r, g = h % RG, h // RG
                    at = (r * GROUPS + g) * P
                    last = n.matmul(PS[HP * r:HP * r + HP, O_BANK, g * P:(g + 1) * P], v_aug[p][:, h, :],
                                    probsT[:, at:at + P], start=True, stop=True)
                return last

            def step(t, p, j):
                edge = isinstance(t, int)

                def scores(banks):
                    for r in banks:
                        if not edge or t > 0:
                            pe.wait_ge(probsT_ready, RG * (t - 1) + r + 1)
                        n.matmul(PS[:, r, :], identb[:, :],
                                 spread(mask[:, :], 1, GROUPS),
                                 start=True, stop=True)
                    pe.wait_ge(q_ready, t + 1)
                    pe.wait_ge(k_ready, t + 1)
                    for g in range(GROUPS):
                        for r in banks:
                            rows = slice(HP * r, HP * r + HP)
                            last = n.matmul(PS[:, r, g * P:(g + 1) * P], qT[p][rows, g, :], kT[p][rows, g, :],
                                            start=False, stop=True, skip_group_check=True)
                            if g == GROUPS - 1:
                                last.then_inc(s_done, 1)

                def keys_to_rows(banks):
                    for r in banks:
                        pe.wait_ge(exp_done, RG * t + r + 1)
                        transposes(probs[:, r * 512:(r + 1) * 512], GROUPS, bank=r).then_inc(probsT_ps, 1)

                def project(u, p, bank, w0, w, done):
                    for k in range(DK):
                        last = n.matmul(PS[:, bank, 0:w], aT[p][:, k, :], wqkv_sb[:, k, w0:w0 + w],
                                        start=(k == 0), stop=(k == DK - 1))
                    last.then_inc(done, 1)
                def keys_and_queries_to_rows(u):
                    pe.wait_ge(qkn_ready, u + 1)
                    flat = qkn[:, :, :].rearrange("p h s -> p (h s)")
                    wait(pe, gexp_ready, t - 2)
                    wait(pe, slot_ready, t - 3)
                    transposes(flat[:, 0:H * HP], GROUPS).then_inc(q_ps, 1)
                    transposes(flat[:, H * HP:2 * H * HP], GROUPS, bank=QK_BANK).then_inc(k_ps, 1)

                def output_projection(u):
                    pe.wait_ge(oT_ready, u + 1)
                    wait(pe, var_f, u)
                    wait(pe, v_ready, u + 3)
                    for k in range(DK):
                        last = n.matmul(PS[:, VY_BANK, D:2 * D], oT[:, k, :], wo_sb[:, k, :],
                                        start=(k == 0), stop=(k == DK - 1))
                    last.then_inc(wo_done, 1)

                def outputs(u):
                    pe.wait_ge(probsT_ready, RG * u + RG)
                    pe.wait_ge(v_ready, u + 1)
                    wait(pe, aT_ready, u + 4)
                    wait(pe, oT_ready, u)
                    values(u, 1 - p, range(H)).then_inc(pv_done, 1)

                def outputs_back(u):
                    pe.wait_ge(o_raw_ready, u + 1)
                    transposes(o_raw, GROUPS, bank=O_BANK).then_inc(o_back, 1)

                def outputs_to_rows(u):
                    pe.wait_ge(o_ready, u + 1)
                    transposes(o_n, DK, bank=O_BANK).then_inc(oT_ps, 1)

                def x2_to_rows(u):
                    wait(pe, q_ready, u + 4)
                    if edge:
                        wait(pe, gexp_ready, u)
                        wait(pe, slot_ready, u - 1)
                    pe.wait_ge(x2_ready, u + 1)
                    transposes(x2[u % 2 if edge else p], DK).then_inc(x2T_ps, 1)

                def gate(u):
                    pe.wait_ge(x2T_ready, u + 1)
                    for k in range(DK):
                        last = n.matmul(PS[:, T_BANK, GATE_AT:GATE_AT + E], x2T[:, k, :], gate_sb[:, k, :],
                                        start=(k == 0), stop=(k == DK - 1))
                    last.then_inc(gate_done, 1)

                def rank(u):
                    pe.wait_ge(chosen_ready, u + 1)
                    wait(pe, sum_ready, u)
                    if edge and t >= B:
                        pe.wait_ge(k_ready, B)
                        pe.wait_ge(slot_ready, u)
                        ranks = late_ranks
                    else:
                        wait(pe, q_ready, t + 2)
                        wait(pe, x2T_ready, t - 1)
                        ranks = PS[:, T_BANK, RANK_AT:RANK_AT + E]
                    n.matmul(ranks, upper[:, :], chosen[1 - p][:, :], start=True, stop=False)
                    n.matmul(ranks, onesb[:, :], chosen_sum[1 - p][:, :], start=False, stop=True).then_inc(rank_done, 1)

                if edge and t >= B:
                    if t == B:
                        output_projection(B - 2)
                        outputs(B - 1)
                        rank(B - 3)
                        outputs_back(B - 1)
                        x2_to_rows(B - 2)
                        outputs_to_rows(B - 1)
                        gate(B - 2)
                        output_projection(B - 1)
                    elif t == B + 1:
                        x2_to_rows(B - 1)
                        gate(B - 1)
                        rank(B - 2)
                    else:
                        rank(B - 1)
                    return
                if edge and t == 0:
                    pe.wait_ge(pool_const, 3)
                    pe.wait_ge(ld_rest, 32)
                if valid(t):
                    scores((0, 1))
                if valid(t - 2):
                    output_projection(t - 2)
                if valid(t):
                    scores((2, 3))
                if valid(t - 1):
                    outputs(t - 1)
                if edge and t == -1:
                    keep_warm(WARM_FIRST)
                if valid(t + 1):
                    keys_and_queries_to_rows(t + 1)
                if valid(t):
                    keys_to_rows((0, 1))
                u = t + 2
                if valid(u):
                    pe.wait_ge(aT_ready, u + 1)
                    wait(pe, k_ready, u)
                    project(u, p, QK_BANK, 0, 2 * D, qk_done)
                if valid(t - 2):
                    x2_to_rows(t - 2)
                if valid(t - 1):
                    outputs_back(t - 1)
                u = t + 1
                if valid(u):
                    wait(pe, v_ready, u)
                    wait(pe, var_f, u - 2)
                    project(u, 1 - p, VY_BANK, 2 * D, D, v_done)
                if valid(t - 3):
                    rank(t - 3)
                if valid(t - 2):
                    gate(t - 2)
                if valid(t):
                    keys_to_rows((2,))
                if valid(t - 1):
                    outputs_to_rows(t - 1)
                if valid(t):
                    keys_to_rows((3,))
                u = t + 3
                if valid(u):
                    pe.wait_ge(a_ready, u + 1)
                    wait(pe, oT_ready, t)
                    wait(pe, aT_ready, u)
                    transposes(a_n[1 - p], DK, bank=O_BANK).then_inc(aT_ps, 1)

            pe.wait_ge(pool_const, 2)
            keep_warm(WARM_START)
            pe.wait_ge(prep_done, 2 + DK)
            attention(pe, step)

            pe.wait_ge(sum_ready, B)
            pe.wait_ge(slot_ready, B)
            n.matmul(counts, onesb[:, :], chosen_sum[0][:, :],
                     start=True, stop=True).then_inc(counts_done, 1)
            pe.wait_ge(trow_loaded, 16)
            for c in range(2):
                last = n.transpose(PS[:, T_BANK, c * P:c * P + NTP], trow[:, :, c], ident[0:NTP, 0:NTP])
            last.then_inc(tab_tr, 1)
            keep_warm(WARM_EXPERTS)
            pe.wait_ge(er_ready, 1)
            pe.wait_ge(slots_read, 1)
            pe.wait_ge(ld_ffn, 16 * 4 * E)

            def x_in_t(t, p):
                pe.wait_ge(xs_ready, t + 1)
                if not isinstance(t, int) or t > 0:
                    pe.wait_ge(xT_ready, t)
                transposes(xg_sb[p], DK).then_inc(xT_tr, 1)

            def up(t, p, e):
                pe.wait_ge(xT_ready, t + 1)
                if not isinstance(t, int) or t > 0:
                    pe.wait_ge(silu_ready, t)
                    pe.wait_ge(hh_ready, t)
                for c in range(4):
                    for k in range(DK):
                        last = n.matmul(PS[:, c, 0:FH], xT_sb[p][:, k, :],
                                        w13_sb[:, bass.ds(e, 1), k, c * FH:(c + 1) * FH],
                                        start=(k == 0), stop=(k == DK - 1))
                last.then_inc(w13_done, 1)

            def h_t(t, p):
                pe.wait_ge(hh_ready, t + 1)
                if not isinstance(t, int) or t > 0:
                    pe.wait_ge(hT_a_ready, t)
                    pe.wait_ge(hT_v_ready, t)
                for i in range(FK):
                    w = min(P, F - i * P)
                    last = n.transpose(PS[0:w, 4 + i // 4, i % 4 * P:(i % 4 + 1) * P],
                                       h_sb[p][:, i * P:i * P + w], ident[:, :])
                last.then_inc(hT_tr, 1)

            def down(t, p, e):
                pe.wait_ge(hT_a_ready, t + 1)
                pe.wait_ge(hT_v_ready, t + 1)
                if not isinstance(t, int) or t > 0:
                    pe.wait_ge(y_ready, t)
                for i in range(FK):
                    w = min(P, F - i * P)
                    last = n.matmul(PS[:, 7, 0:D], hT_sb[p][0:w, i, :], w2_sb[0:w, bass.ds(e, 1), i, :],
                                    start=(i == 0), stop=(i == FK - 1))
                last.then_inc(w2_done, 1)

            def expert_of(t):
                return pe.value_load(er_i[0:1, bass.ds(t, 1)], min_val=0, max_val=E - 1)

            def expert_step(t, p, j):
                up(t, p, expert_of(t))
                x_in_t(t + 1, 1 - p)
                down(t - 1, 1 - p, expert_of(t - 1))
                h_t(t, p)
            x_in_t(0, 0)
            up(0, 0, expert_of(0))
            x_in_t(1, 1)
            h_t(0, 0)
            experts(pe, 1, 3, expert_step)
            down(NT - 1, 0, expert_of(NT - 1))


def kernel(**inputs):
    import concourse.bacc as bacc
    import numpy as np
    from concourse.bass_utils import run_bass_kernel_spmd

    a = {name: np.asarray(v) for name, v in inputs.items()}

    def padded(v):
        return np.tile(np.concatenate([v, np.zeros(HP - HD, v.dtype)]), RG)

    bias_row = np.zeros(D, np.float32)
    bias_row[0:E] = a["L0_ffn_expert_bias"]
    arrays = {
        "ids": np.ascontiguousarray(a["x"].T),
        "types": np.ascontiguousarray(a["mask_BS_i1_0"].T),
        "word": a["L0_tok_word_emb"],
        "rows": np.concatenate([a["L0_tok_pos_emb"], a["L0_tok_type_emb"], a["L0_tok_gamma"][None],
                                a["L0_tok_beta"][None], a["L0_attn_bo"][None], bias_row[None]]),
        "w_qkv": np.concatenate([a["L0_attn_Wq"], a["L0_attn_Wk"], a["L0_attn_Wv"]], axis=1),
        "w_o": a["L0_attn_Wo"],
        "head_cols": np.stack([padded(a[f"L0_attn_{n}"]) for n in ("qln_w", "qln_b", "kln_w", "kln_b")], axis=1),
        "gate_t": np.ascontiguousarray(a["L0_ffn_gate_w"].T),
        "w1": a["L0_ffn_w1"],
        "w3": a["L0_ffn_w3"],
        "w2": a["L0_ffn_w2"],
    }
    arrays = {name: np.ascontiguousarray(v) for name, v in arrays.items()}
    nc = bacc.Bacc("TRN2", target_bir_lowering=False, num_devices=1)
    args = [nc.dram_tensor(f"{name}_dram", v.shape, mybir.dt.from_np(v.dtype), kind="ExternalInput").ap()
            for name, v in arrays.items()]
    out = nc.dram_tensor("out_dram", (TOK + P, D), mybir.dt.float32, kind="ExternalOutput").ap()
    build_tower(nc, *args, out)
    r = run_bass_kernel_spmd(nc, [{f"{name}_dram": v for name, v in arrays.items()}], core_ids=[0])
    return r.results[0]["out_dram"][0:TOK].reshape(B, P, D)
```
